# Optimizing a Trainium2 kernel written in Bass

```python
import numpy as np
import jax
import jax.numpy as jnp

def _softmax(x, axis=-1):
    return jax.nn.softmax(x, axis=axis)

def _gelu(x):
    return jax.nn.gelu(x, approximate=True)

def _silu(x):
    return jax.nn.silu(x)

def _sigmoid(x):
    return jax.nn.sigmoid(x)

def _layernorm(x, axis=-1, eps=1e-05):
    m = jnp.mean(x, axis=axis, keepdims=True)
    v = jnp.var(x, axis=axis, keepdims=True)
    return (x - m) / jnp.sqrt(v + eps)

def _scatter_add(tgt, idx, src, axis=0):
    return tgt.at[idx].add(src)

def _segment_sum(src, seg, n):
    return jax.ops.segment_sum(src, seg, n)
kernel_name = 'mk_gnn_resnorm_d4_gnn_r16_a20545'

def setup_inputs(seed: int=0):
    np.random.seed(seed)
    _w = jnp.asarray

    def _rec_inputs():
        import jax
        import jax.numpy as jnp
        _gk = jax.random.key(seed)
        x = -0.0003713 + 1 * jax.random.normal(jax.random.fold_in(_gk, 1), (6250, 256), jnp.float32)
        src = jax.random.randint(jax.random.fold_in(_gk, 2), (100000,), 0, 6250, jnp.int32)
        dst = jax.random.randint(jax.random.fold_in(_gk, 3), (100000,), 0, 6250, jnp.int32)
        _o = jnp.argsort(dst, stable=True)
        src = src[_o]
        dst = dst[_o]
        edge_attr_2 = jax.random.uniform(jax.random.fold_in(_gk, 12), (100000, 2), jnp.float32, 0.0, 1)
        edge_weight = jax.random.uniform(jax.random.fold_in(_gk, 14), (100000,), jnp.float32, 0.0, 1)
        return (x, src, dst, edge_attr_2, edge_weight)
    x, src, dst, edge_attr_2, edge_weight = _rec_inputs()

    def _L0_gnn_setup():
        import jax, jax.numpy as jnp
        import numpy as np
        N_NODES = 3125
        N_EDGES = 100000
        H_SIZE = 256
        HEADS = 8
        HEAD_DIM = H_SIZE // HEADS
        NEG_SLOPE = 0.2
        key = jax.random.key(seed)
        k_x, k_e, k_w, k_as, k_ad, k_b = jax.random.split(key, 6)
        x = jax.random.normal(k_x, (N_NODES, H_SIZE), dtype=jnp.float32)
        edge_index = jax.random.randint(k_e, (2, N_EDGES), 0, N_NODES, dtype=jnp.int64)
        scale = 1.0 / np.sqrt(H_SIZE)
        W = jax.random.normal(k_w, (H_SIZE, HEADS, HEAD_DIM), dtype=jnp.float32) * scale
        att_src = jax.random.normal(k_as, (HEADS, HEAD_DIM), dtype=jnp.float32) * scale
        att_dst = jax.random.normal(k_ad, (HEADS, HEAD_DIM), dtype=jnp.float32) * scale
        bias = jnp.zeros((H_SIZE,), dtype=jnp.float32)
        return {'x': x, 'edge_index': edge_index, 'W': W, 'att_src': att_src, 'att_dst': att_dst, 'bias': bias}
    _L0_gnn_all = _L0_gnn_setup()
    _L0_gnn_in = {k: v for k, v in _L0_gnn_all.items() if k in ('W', 'att_src', 'att_dst', 'bias')}
    del _L0_gnn_all

    def _L1_gnn_setup():
        import jax, jax.numpy as jnp
        import numpy as np
        LN_EPS = 1e-05

        def layer_norm(h, gamma, beta):
            mu = jnp.mean(h, axis=-1, keepdims=True)
            var = jnp.mean(jnp.square(h - mu), axis=-1, keepdims=True)
            return (h - mu) * jax.lax.rsqrt(var + LN_EPS) * gamma + beta

        def gcn_conv(x, src, dst, W, b, n_nodes):
            h = x @ W
            deg = jax.ops.segment_sum(jnp.ones_like(src, dtype=h.dtype), dst, num_segments=n_nodes)
            dinv = jax.lax.rsqrt(jnp.maximum(deg, 1.0))
            norm = dinv[src] * dinv[dst]
            msg = h[src] * norm[:, None]
            return jax.ops.segment_sum(msg, dst, num_segments=n_nodes) + b
        key = jax.random.key(seed)
        ks = jax.random.split(key, 8)
        N, E, Cin, Ch, Cout = (625, 10000, 256, 512, 256)
        x = jax.random.normal(ks[0], (N, Cin), dtype=jnp.float32)
        edge_index = jax.random.randint(ks[1], (2, E), 0, N, dtype=jnp.int64)
        W1 = jax.random.normal(ks[2], (Cin, Ch), dtype=jnp.float32) * (1.0 / np.sqrt(Cin))
        b1 = jnp.zeros((Ch,), dtype=jnp.float32)
        gamma1 = jnp.ones((Ch,), dtype=jnp.float32)
        beta1 = jnp.zeros((Ch,), dtype=jnp.float32)
        W2 = jax.random.normal(ks[3], (Ch, Cout), dtype=jnp.float32) * (1.0 / np.sqrt(Ch))
        b2 = jnp.zeros((Cout,), dtype=jnp.float32)
        gamma2 = jnp.ones((Cout,), dtype=jnp.float32)
        beta2 = jnp.zeros((Cout,), dtype=jnp.float32)
        return {'x': x, 'edge_index': edge_index, 'W1': W1, 'b1': b1, 'gamma1': gamma1, 'beta1': beta1, 'W2': W2, 'b2': b2, 'gamma2': gamma2, 'beta2': beta2}
    _L1_gnn_all = _L1_gnn_setup()
    _L1_gnn_in = {k: v for k, v in _L1_gnn_all.items() if k in ('W1', 'b1', 'gamma1', 'beta1', 'W2', 'b2', 'gamma2', 'beta2')}
    del _L1_gnn_all

    def _L2_gnn_setup():
        import jax, jax.numpy as jnp
        import numpy as np
        N_NODES = 6250
        N_EDGES = 100000
        IN_FEATS = 256
        OUT_FEATS = 256
        key = jax.random.key(seed)
        k_h, k_norm, k_w, k_b, k_src, k_dst = jax.random.split(key, 6)
        stdv = 1.0 / np.sqrt(OUT_FEATS)
        return {'h': jax.random.normal(k_h, (N_NODES, IN_FEATS), dtype=jnp.float32), 'sym_norm': jax.random.uniform(k_norm, (N_EDGES,), dtype=jnp.float32), 'W': jax.random.uniform(k_w, (IN_FEATS, OUT_FEATS), dtype=jnp.float32, minval=-stdv, maxval=stdv), 'b': jax.random.uniform(k_b, (OUT_FEATS,), dtype=jnp.float32, minval=-stdv, maxval=stdv), 'src': jax.random.randint(k_src, (N_EDGES,), 0, N_NODES, dtype=jnp.int32), 'dst': jax.random.randint(k_dst, (N_EDGES,), 0, N_NODES, dtype=jnp.int32)}
    _L2_gnn_all = _L2_gnn_setup()
    _L2_gnn_in = {k: v for k, v in _L2_gnn_all.items() if k in ('W', 'b')}
    del _L2_gnn_all

    def _L3_gnn_setup():
        import jax, jax.numpy as jnp
        import numpy as np
        N_NODES = 6250
        N_EDGES = 100000
        IN_FEATS = 256
        OUT_FEATS = 64
        NUM_HEADS = 4
        key = jax.random.key(seed)
        k_h, k_adj, k_dir, k_wf, k_wr, k_af = jax.random.split(key, 6)
        h = jax.random.normal(k_h, (N_NODES, IN_FEATS), dtype=jnp.float32)
        adj = jax.random.randint(k_adj, (2, N_EDGES), 0, N_NODES, dtype=jnp.int64)
        bit = jax.random.randint(k_dir, (N_EDGES,), 0, 2).astype(jnp.float32)
        direction = jnp.stack([bit, 1.0 - bit], axis=1)
        s_w = float(np.sqrt(6.0 / (IN_FEATS + OUT_FEATS)))
        s_a = float(np.sqrt(6.0 / (NUM_HEADS + OUT_FEATS)))
        W_forward = jax.random.uniform(k_wf, (OUT_FEATS, IN_FEATS), jnp.float32, -s_w, s_w)
        W_reverse = jax.random.uniform(k_wr, (OUT_FEATS, IN_FEATS), jnp.float32, -s_w, s_w)
        attn_forward = jax.random.uniform(k_af, (1, NUM_HEADS, OUT_FEATS), jnp.float32, -s_a, s_a)
        return {'h': h, 'adj': adj, 'direction': direction, 'W_forward': W_forward, 'W_reverse': W_reverse, 'attn_forward': attn_forward}
    _L3_gnn_all = _L3_gnn_setup()
    _L3_gnn_in = {k: v for k, v in _L3_gnn_all.items() if k in ('W_forward', 'W_reverse', 'attn_forward')}
    del _L3_gnn_all
    return {'x': x, 'src': src, 'dst': dst, 'edge_attr_2': edge_attr_2, 'edge_weight': edge_weight, 'L0_gnn_W': _L0_gnn_in['W'], 'L0_gnn_att_src': _L0_gnn_in['att_src'], 'L0_gnn_att_dst': _L0_gnn_in['att_dst'], 'L0_gnn_bias': _L0_gnn_in['bias'], 'L1_gnn_W1': _L1_gnn_in['W1'], 'L1_gnn_b1': _L1_gnn_in['b1'], 'L1_gnn_gamma1': _L1_gnn_in['gamma1'], 'L1_gnn_beta1': _L1_gnn_in['beta1'], 'L1_gnn_W2': _L1_gnn_in['W2'], 'L1_gnn_b2': _L1_gnn_in['b2'], 'L1_gnn_gamma2': _L1_gnn_in['gamma2'], 'L1_gnn_beta2': _L1_gnn_in['beta2'], 'L2_gnn_W': _L2_gnn_in['W'], 'L2_gnn_b': _L2_gnn_in['b'], 'L3_gnn_W_forward': _L3_gnn_in['W_forward'], 'L3_gnn_W_reverse': _L3_gnn_in['W_reverse'], 'L3_gnn_attn_forward': _L3_gnn_in['attn_forward']}

def reference(x, src, dst, edge_attr_2, edge_weight, L0_gnn_W, L0_gnn_att_src, L0_gnn_att_dst, L0_gnn_bias, L1_gnn_W1, L1_gnn_b1, L1_gnn_gamma1, L1_gnn_beta1, L1_gnn_W2, L1_gnn_b2, L1_gnn_gamma2, L1_gnn_beta2, L2_gnn_W, L2_gnn_b, L3_gnn_W_forward, L3_gnn_W_reverse, L3_gnn_attn_forward):
    import jax
    import jax.numpy as jnp

    def _L0_gnn_ref(x, edge_index, W, att_src, att_dst, bias):
        import jax, jax.numpy as jnp
        import numpy as np
        N_NODES = 3125
        N_EDGES = 100000
        H_SIZE = 256
        HEADS = 8
        HEAD_DIM = H_SIZE // HEADS
        NEG_SLOPE = 0.2
        'GATConv (concat heads) -> relu -> dropout(eval=identity).\n\n            x: [N, F]; edge_index: [2, E] with (src=row0, dst=row1) meaning message j->i.\n            '
        N = x.shape[0]
        h = jnp.einsum('nf,fhd->nhd', x, W)
        a_src = jnp.sum(h * att_src, axis=-1)
        a_dst = jnp.sum(h * att_dst, axis=-1)
        src = edge_index[0]
        dst = edge_index[1]
        e = jax.nn.leaky_relu(a_src[src] + a_dst[dst], NEG_SLOPE)
        e_max = jax.ops.segment_max(e, dst, num_segments=N)
        e_exp = jnp.exp(e - e_max[dst])
        denom = jax.ops.segment_sum(e_exp, dst, num_segments=N)
        alpha = e_exp / (denom[dst] + 1e-16)
        msg = h[src] * alpha[:, :, None]
        out = jax.ops.segment_sum(msg, dst, num_segments=N)
        out = out.reshape(N, -1) + bias
        return jax.nn.relu(out)

    def _L1_gnn_ref(x, edge_index, W1, b1, gamma1, beta1, W2, b2, gamma2, beta2):
        import jax, jax.numpy as jnp
        import numpy as np
        LN_EPS = 1e-05

        def layer_norm(h, gamma, beta):
            mu = jnp.mean(h, axis=-1, keepdims=True)
            var = jnp.mean(jnp.square(h - mu), axis=-1, keepdims=True)
            return (h - mu) * jax.lax.rsqrt(var + LN_EPS) * gamma + beta

        def gcn_conv(x, src, dst, W, b, n_nodes):
            h = x @ W
            deg = jax.ops.segment_sum(jnp.ones_like(src, dtype=h.dtype), dst, num_segments=n_nodes)
            dinv = jax.lax.rsqrt(jnp.maximum(deg, 1.0))
            norm = dinv[src] * dinv[dst]
            msg = h[src] * norm[:, None]
            return jax.ops.segment_sum(msg, dst, num_segments=n_nodes) + b
        n = x.shape[0]
        loops = jnp.arange(n, dtype=edge_index.dtype)
        src = jnp.concatenate([edge_index[0], loops])
        dst = jnp.concatenate([edge_index[1], loops])
        h = gcn_conv(x, src, dst, W1, b1, n)
        h = jax.nn.relu(layer_norm(h, gamma1, beta1))
        g = gcn_conv(h, src, dst, W2, b2, n)
        g = jax.nn.relu(layer_norm(g, gamma2, beta2))
        return g

    def _L2_gnn_ref(h, sym_norm, W, b, src, dst):
        import jax, jax.numpy as jnp
        import numpy as np
        N_NODES = 6250
        N_EDGES = 100000
        IN_FEATS = 256
        OUT_FEATS = 256
        n_nodes = h.shape[0]
        hw = jnp.matmul(h, W)
        msg = hw[src] * sym_norm[:, None]
        agg = jax.ops.segment_sum(msg, dst, num_segments=n_nodes)
        return jax.nn.relu(agg + b)

    def _L3_gnn_ref(h, adj, direction, W_forward, W_reverse, attn_forward):
        import jax, jax.numpy as jnp
        import numpy as np
        N_NODES = 6250
        N_EDGES = 100000
        IN_FEATS = 256
        OUT_FEATS = 64
        NUM_HEADS = 4
        N = h.shape[0]
        H = attn_forward.shape[1]
        h_fwd = h @ W_forward.T
        h_rev = h @ W_reverse.T
        src, dst = (adj[0], adj[1])
        messages = h_fwd[src] * direction[:, 0:1] + h_rev[src] * direction[:, 1:2]
        scores = jnp.einsum('ef,hf->eh', messages, attn_forward[0])
        scores = jax.nn.leaky_relu(scores, negative_slope=0.2)
        exp_scores = jnp.exp(scores - scores.max(axis=0, keepdims=True))
        sum_exp = jax.ops.segment_sum(exp_scores, dst, num_segments=N)
        norm = exp_scores / (sum_exp[dst] + 1e-10)
        outs = [jax.ops.segment_sum(messages * norm[:, hd:hd + 1], dst, num_segments=N) for hd in range(H)]
        out = jnp.stack(outs, axis=1)
        return out.reshape(N, -1)
    edge_index = jnp.stack([src, dst])
    x = _layernorm(x + _L0_gnn_ref(x, edge_index, L0_gnn_W, L0_gnn_att_src, L0_gnn_att_dst, L0_gnn_bias), axis=-1)
    x = _layernorm(x + _L1_gnn_ref(x, edge_index, L1_gnn_W1, L1_gnn_b1, L1_gnn_gamma1, L1_gnn_beta1, L1_gnn_W2, L1_gnn_b2, L1_gnn_gamma2, L1_gnn_beta2), axis=-1)
    x = _layernorm(x + _L2_gnn_ref(x, edge_weight, L2_gnn_W, L2_gnn_b, src, dst), axis=-1)
    x = _layernorm(x + _L3_gnn_ref(x, edge_index, edge_attr_2, L3_gnn_W_forward, L3_gnn_W_reverse, L3_gnn_attn_forward), axis=-1)
    return x

_drawn_inputs = setup_inputs


def setup_inputs(seed=0):
    import zlib

    import numpy as np

    out = dict(_drawn_inputs(seed))
    spreads = {'L0_gnn_bias': (0.0, 0.1),
     'L1_gnn_b1': (0.0, 0.1),
     'L1_gnn_gamma1': (1.0, 0.2),
     'L1_gnn_beta1': (0.0, 0.1),
     'L1_gnn_b2': (0.0, 0.1),
     'L1_gnn_gamma2': (1.0, 0.2),
     'L1_gnn_beta2': (0.0, 0.1)}
    factors = {'L0_gnn_att_dst': 5.086, 'L2_gnn_b': 3.136}
    for name, (base, spread) in spreads.items():
        noise = np.random.default_rng([zlib.crc32(name.encode()), seed]).standard_normal(out[name].shape)
        drawn = base * np.exp(spread * noise) if base else spread * noise
        out[name] = jnp.asarray(drawn.astype(out[name].dtype))
    for name, factor in factors.items():
        out[name] = (out[name] * factor).astype(out[name].dtype)
    return out
```

```python
from contextlib import ExitStack

import numpy as np

import concourse.bass as bass
from concourse import mybir

F32 = mybir.dt.float32
I32 = mybir.dt.int32
ALU = mybir.AluOpType
ACT = mybir.ActivationFunctionType
AXX = mybir.AxisListType.X

P = 128
NODES = 6250
EDGES = 100000
FEAT = 256
NODE_TILES = -(-NODES // P)
NODES_PAD = NODE_TILES * P
FULL_TILES = NODES // P
TAIL_ROWS = NODES - FULL_TILES * P
CHUNKS = -(-EDGES // P)
EDGES_PAD = CHUNKS * P
STEPS = CHUNKS + NODE_TILES - 1
SEGS = 16
RUN = -(-STEPS // SEGS)
STEPS_PAD = SEGS * RUN
STEP_BLOCKS = -(-STEPS_PAD // P)
HEADS0 = 8
HEAD0_DIM = FEAT // HEADS0
HEADS3 = 4
OUT3 = 64
HIDDEN = 512
ACC_W = FEAT + 2 * HEADS0
LOW = -1.0e38
LN_EPS = 1e-5
JUNK_NODE = NODES_PAD - 1


class Engine:

    def __init__(self, sem):
        self.sem, self.count, self.queue, self.seen = sem, 0, [], {}

    def wait(self, *tokens):
        for sem, value in tokens:
            if self.seen.get(id(sem), 0) < value:
                self.seen[id(sem)] = value
                self.queue.append(lambda e, s=sem, v=value: e.wait_ge(s, v))

    def do(self, make, after=()):
        self.wait(*after)
        self.count += 1
        self.queue.append(lambda e: make(e).then_inc(self.sem, 1))
        return (self.sem, self.count)

    def dma(self, make, done, after=()):
        self.wait(*after)
        done[1] += 16
        self.queue.append(lambda e: make(e).then_inc(done[0], 16))
        return (done[0], done[1])

    def plain(self, make):
        self.queue.append(make)

    def last(self):
        return (self.sem, self.count)

    def replay(self, e):
        for step in self.queue:
            step(e)


def pipeline(n, stages):
    for i in range(n + len(stages) - 1):
        for k in range(len(stages) - 1, -1, -1):
            if 0 <= i - k < n:
                stages[k](i - k)


def build(nc, io):
    ctx = ExitStack()
    with ctx:
        def sb(name, width, dt=F32, rows=P):
            return ctx.enter_context(nc.sbuf_tensor(name, [rows, width], dt))

        def sem(name):
            return ctx.enter_context(nc.semaphore(name))

        def dram(name, shape, dt=F32):
            return nc.dram_tensor(name, shape, dt, kind="Internal").ap()

        reg_x = sb("reg_x", max(NODE_TILES * FEAT, 2 * RUN * P))
        reg_acc = sb("reg_acc", NODE_TILES * ACC_W)
        reg_a = sb("reg_a", STEPS_PAD * HEADS0)
        reg_b = sb("reg_b", STEPS_PAD * (HEADS0 + 1))
        reg_w = sb("reg_w", 7 * HIDDEN)
        src_idx = sb("src_idx", STEPS_PAD, I32)
        dst_loc = sb("dst_loc", STEPS_PAD)
        edge_w = sb("edge_w", STEPS_PAD)
        attr0 = sb("attr0", STEPS_PAD)
        attr1 = sb("attr1", STEPS_PAD)
        cap = sb("cap", STEPS_PAD)[:, :]
        tile_row = sb("tile_row", STEPS_PAD, I32, rows=1)
        ident = sb("ident", P)
        iota_row = sb("iota_row", P)
        adst = sb("adst", NODE_TILES * HEADS0)
        dinv = sb("dinv", NODE_TILES)
        small = sb("small", 512)
        psum = [ctx.enter_context(nc.psum_tensor(f"bank{k}", [P, 512], F32)) for k in range(8)]

        tab_h0 = dram("tab_h0", [NODES_PAD, FEAT])
        tab_a0 = dram("tab_a0", [NODES_PAD, HEADS0])
        tab_x1 = dram("tab_x1", [NODES_PAD, FEAT])
        tab_h2 = dram("tab_h2", [NODES_PAD, FEAT])
        tab_x2 = dram("tab_x2", [NODES_PAD, FEAT])
        tab_h3 = dram("tab_h3", [NODES_PAD, 2 * OUT3])
        tab_a3 = dram("tab_a3", [NODES_PAD, 2 * HEADS3])
        tile_dram = dram("tile_dram", [STEP_BLOCKS * P, 1], I32)

        pe, dve, act, pool, sp = (Engine(sem(f"s_{n}")) for n in ("pe", "dve", "act", "pool", "sp"))
        engines = (pe, dve, act, pool, sp)
        load_done = [sem("s_load"), 0]
        load2_done = [sem("s_load2"), 0]
        store_done = [sem("s_store"), 0]
        table_done = [sem("s_table"), 0]
        n_gather = 12
        gather_done = [[sem(f"s_gather{k}"), 0] for k in range(n_gather)]
        counters = [load_done, load2_done, store_done, table_done] + gather_done

        def phase_end():
            tokens = [e.last() for e in engines] + [tuple(c) for c in counters]
            for e in engines:
                e.wait(*tokens)

        def tt(out, a, b, op, after=(), eng=None):
            return (eng or dve).do(lambda e: e.tensor_tensor(out, a, b, op), after)

        def ts(out, a, s1, s2, op0, op1=None, after=()):
            if op1 is None:
                return dve.do(lambda e: e.tensor_scalar(out, a, s1, None, op0), after)
            return dve.do(lambda e: e.tensor_scalar(out, a, s1, s2, op0, op1), after)

        def stt(out, a, s, b, op0, op1, after=()):
            return dve.do(lambda e: e.scalar_tensor_tensor(out=out, in0=a, scalar=s, in1=b, op0=op0, op1=op1), after)

        def copy(eng, out, a, after=()):
            if eng is act:
                return act.do(lambda e: e.copy(out, a), after)
            return eng.do(lambda e: e.tensor_copy(out, a), after)

        def activate(out, a, fn, after=(), **kw):
            return act.do(lambda e: e.activation(out, a, fn, **kw), after)

        def mm(out, lhs_t, rhs, start=True, stop=True, after=()):
            return pe.do(lambda e: e.matmul(out, lhs_t, rhs, start=start, stop=stop), after)

        def transpose(out, a, after=()):
            n = a.shape[0]
            return pe.do(lambda e: e.transpose(out, a, ident[0:n, 0:n]), after)

        def load(out, a, after=()):
            return sp.dma(lambda e: e.dma_start(out, a), load_done, after)

        def gather(out, table, t, done, after=()):
            return pool.dma(lambda e: e.indirect_dma_start(
                out, None, table, bass.IndirectOffsetOnAxis(ap=src_idx[:, t:t + 1], axis=0)), done, after)

        def node_rows(table, a, b):
            return table.rearrange("(t p) f -> p t f", p=P)[:, a:b, :]

        def bcast(ap, axis, shape):
            return ap.unsqueeze(axis).to_broadcast(shape)

        x_sb = reg_x[:, 0:NODE_TILES * FEAT].rearrange("p (t f) -> p t f", f=FEAT)
        acc = reg_acc[:, :].rearrange("p (t f) -> p t f", f=ACC_W)

        small_i = small[:, 0:P].bitcast(I32)
        t_iota = pool.do(lambda e: e.iota(small_i, pattern=[[1, P]], base=0, channel_multiplier=0))
        t_part = pool.do(lambda e: e.iota(small[:, P:P + 1].bitcast(I32), pattern=[[0, 1]], base=0,
                                          channel_multiplier=1))
        step_i = small[:, 144:144 + STEP_BLOCKS].bitcast(I32)
        t_step = pool.do(lambda e: e.iota(step_i, pattern=[[P, STEP_BLOCKS]], base=0, channel_multiplier=1))
        chunk_i = reg_a[0:1, 0:CHUNKS].bitcast(I32)
        t_chunk = pool.do(lambda e: e.iota(chunk_i, pattern=[[1, CHUNKS]], base=1, channel_multiplier=0))
        copy(dve, iota_row[:, :], small_i, [t_iota])
        part = small[:, 130:131]
        t = copy(dve, part, small[:, P:P + 1].bitcast(I32), [t_part])
        ts(ident[:, :], iota_row[:, :], part, None, ALU.is_equal, after=[t])
        step_no = small[:, 160:160 + STEP_BLOCKS]
        copy(dve, step_no, step_i, [t_step])
        ones_row = small[0:1, 200:200 + P]
        dve.do(lambda e: e.memset(ones_row, 1.0))

        last_dst = reg_a[0:1, 800:800 + CHUNKS].bitcast(I32)
        ends = io["edge_ints"][:, 2 * P - 1:2 * P].rearrange("c k -> k c")
        t = sp.dma(lambda e: e.dma_start(last_dst, ends, allow_slow_non_contiguous=True), load_done)
        last_tile = reg_a[0:1, 1600:1600 + CHUNKS].bitcast(I32)
        t = dve.do(lambda e: e.tensor_scalar(last_tile, last_dst, 7, None, ALU.arith_shift_right), [t])
        bound = reg_a[0:1, 2400:2400 + CHUNKS]
        t = tt(bound, last_tile, chunk_i, ALU.add, [t, t_chunk])
        half = CHUNKS // 2
        mm(psum[0][:, 0:half], ones_row, bound[:, 0:half], after=[t])
        t = mm(psum[1][:, 0:CHUNKS - half], ones_row, bound[:, half:CHUNKS])
        bounds = reg_a[:, 3200:3200 + CHUNKS]
        copy(dve, bounds[:, 0:half], psum[0][:, 0:half], [t])
        t = copy(dve, bounds[:, half:CHUNKS], psum[1][:, 0:CHUNKS - half])
        chunk_of = small[:, 170:170 + STEP_BLOCKS]
        hits = reg_a[:, 4000:4000 + CHUNKS]
        for b in range(STEP_BLOCKS):
            t = dve.do(lambda e, b=b: e.tensor_scalar(hits, bounds, step_no[:, b:b + 1], 0.0, ALU.is_le, ALU.add,
                                                      accum_out=chunk_of[:, b:b + 1]), [t])
        t = ts(chunk_of, chunk_of, float(CHUNKS - 1), None, ALU.min, after=[t])
        tile_of = small[:, 180:180 + STEP_BLOCKS]
        chunk_idx = small[:, 190:190 + STEP_BLOCKS].bitcast(I32)
        t_idx = copy(dve, chunk_idx, chunk_of, [t])
        t = tt(tile_of, step_no, chunk_of, ALU.subtract, [t])
        first_node = small[:, 330:330 + STEP_BLOCKS]
        t_first = ts(first_node, tile_of, float(P), None, ALU.mult, after=[t])
        tile_i = small[:, 340:340 + STEP_BLOCKS].bitcast(I32)
        t = ts(tile_i, tile_of, float(NODE_TILES - 1), None, ALU.min, after=[t])
        t = sp.dma(lambda e: e.dma_start(tile_dram.rearrange("(b p) k -> p (b k)", p=P), tile_i,
                                              allow_slow_non_contiguous=True), store_done, [t])
        t = sp.dma(lambda e: e.dma_start(tile_row[:, :], tile_dram[0:STEPS_PAD, :].rearrange("s k -> k s")),
                   load2_done, [t])

        NI, NF = 4, 3
        ints = reg_x[:, 0:STEP_BLOCKS * NI * P].bitcast(I32).rearrange("p (b f) -> p b f", b=STEP_BLOCKS)
        flts = reg_x[:, STEP_BLOCKS * NI * P:STEP_BLOCKS * (NI + NF) * P].rearrange("p (b f) -> p b f", b=STEP_BLOCKS)
        conv = reg_acc[:, 0:STEP_BLOCKS * NI * P].rearrange("p (b f) -> p b f", b=STEP_BLOCKS)
        for b in range(STEP_BLOCKS):
            for out, table in ((ints[:, b, :], io["edge_ints"]), (flts[:, b, :], io["edge_floats"])):
                t_rows = pool.dma(lambda e, out=out, table=table, b=b: e.indirect_dma_start(
                    out, None, table, bass.IndirectOffsetOnAxis(ap=chunk_idx[:, b:b + 1], axis=0)),
                    table_done, [t_idx])
        dst_before = reg_b[:, 0:STEPS_PAD]
        dst_behind = reg_b[:, STEPS_PAD:2 * STEPS_PAD]
        flag = reg_b[:, 2 * STEPS_PAD:3 * STEPS_PAD]
        is_valid = reg_b[:, 3 * STEPS_PAD:4 * STEPS_PAD]
        start_mask = reg_b[:, 4 * STEPS_PAD:5 * STEPS_PAD]
        end_mask = reg_b[:, 5 * STEPS_PAD:6 * STEPS_PAD]
        freed = {}
        for b in range(STEP_BLOCKS):
            w = min(P, STEPS_PAD - b * P)
            cols = slice(b * P, b * P + w)
            t_src = copy(dve, conv[:, b, 0:P], ints[:, b, 0:P], [t_rows])
            t_dst = ts(conv[:, b, P:4 * P], ints[:, b, P:4 * P], first_node[:, b:b + 1], None, ALU.subtract,
                       after=[t_first])
            at = flts[:, b, 0:2 * P].rearrange("p (j k) -> p k j", k=2)
            jobs = [(conv[:, b, 0:P], src_idx), (conv[:, b, P:2 * P], dst_loc),
                    (conv[:, b, 2 * P:3 * P], dst_before), (conv[:, b, 3 * P:4 * P], dst_behind),
                    (at[:, 0, :], attr0), (at[:, 1, :], attr1), (flts[:, b, 2 * P:3 * P], edge_w)]
            for n, (a, out) in enumerate(jobs):
                k = (b * len(jobs) + n) % 8
                t = transpose(psum[k][:, 0:P], a, [t_dst, t_rows] + ([freed[k]] if k in freed else []))
                freed[k] = t_tab = copy(dve, out[:, cols], psum[k][:, 0:w], [t])
        t = ts(flag, dst_loc[:, :], 0.0, None, ALU.is_ge, after=[t_tab])
        t = stt(is_valid, dst_loc[:, :], float(P), flag, ALU.is_lt, ALU.mult, [t])
        ts(cap, is_valid, -2.0 * LOW, LOW, ALU.mult, ALU.add, after=[t])
        for other, mask in ((dst_before, start_mask), (dst_behind, end_mask)):
            t = tt(flag, dst_loc[:, :], other, ALU.not_equal, [dve.last()])
            t = stt(mask, flag, LOW, is_valid, ALU.mult, ALU.mult, [t])
        phase_end()

        x_rows = io["x"][0:FULL_TILES * P, :].rearrange("(t p) f -> p t f", p=P)

        def load_x(after=()):
            t = dve.do(lambda e: e.memset(x_sb[:, FULL_TILES, :], 0.0), after)
            load(x_sb[0:TAIL_ROWS, FULL_TILES, :], io["x"][FULL_TILES * P:NODES, :], [t])
            return load(x_sb[:, 0:FULL_TILES, :], x_rows, after)

        def score_weights(w_ext, w, att, where, after):
            prod = reg_a[:, 0:2 * FEAT].rearrange("p (k f) -> p k f", k=2)
            t = tt(prod, w, bcast(att, 1, [P, 2, FEAT]), ALU.mult, after)
            return dve.do(lambda e: e.tensor_reduce(
                w_ext[:, :, where:where + HEADS0], prod.rearrange("p k (h d) -> p k h d", h=HEADS0), AXX, ALU.add), [t])

        w0 = reg_w[:, 0:2 * ACC_W].rearrange("p (k f) -> p k f", k=2)
        att = reg_w[:, 2 * ACC_W:2 * ACC_W + 2 * FEAT]
        w_rows = io["w0"].rearrange("(k p) f -> p k f", p=P)
        load(w0[:, :, 0:FEAT], w_rows)
        for n, name in enumerate(("att_src", "att_dst")):
            load(att[:, n * FEAT:(n + 1) * FEAT], io[name].partition_broadcast(P))
        t = load_x()
        t = score_weights(w0, w0[:, :, 0:FEAT], att[:, 0:FEAT], FEAT, [t, tuple(load_done)])
        t_w0 = score_weights(w0, w0[:, :, 0:FEAT], att[:, FEAT:2 * FEAT], FEAT + HEADS0, [t])

        def matmul_stages(source, k_chunks, weights, width, turned, ready, banks=(0, 1, 2, 3)):
            t_turn, t_copy, t_mm, used = {}, {}, {}, {}
            two = turned.rearrange("p (s f) -> p s f", s=2)

            def turn(j):
                for k in range(k_chunks):
                    t_turn[j] = transpose(psum[banks[j % 2]][:, k * P:(k + 1) * P], source(j)[:, k * P:(k + 1) * P],
                                          ready(j) + ([t_copy[j - 2]] if j >= 2 else []))

            def keep(j):
                t_copy[j] = copy(act, two[:, j % 2, :], psum[banks[j % 2]][:, 0:k_chunks * P],
                                 [t_turn[j]] + ([t_mm[j - 2]] if j >= 2 else []))

            def multiply(j):
                for k in range(k_chunks):
                    t_mm[j] = mm(psum[banks[2 + j % 2]][:, 0:width], two[:, j % 2, k * P:(k + 1) * P], weights[:, k, :],
                                 k == 0, k == k_chunks - 1,
                                 [t_copy[j]] + ([used[j - 2]] if j >= 2 else []))

            return turn, keep, multiply, t_mm, used, banks

        turned = reg_a[:, 1024:1024 + 4 * P]
        turn, keep, multiply, t_mm, used, banks = matmul_stages(
            lambda j: x_sb[:, j, :], 2, w0, ACC_W, turned, lambda j: [t_w0, tuple(load_done)])

        def keep_h(j):
            copy(dve, acc[:, j, :], psum[banks[2 + j % 2]][:, 0:ACC_W], [t_mm[j]])
            used[j] = copy(dve, adst[:, j * HEADS0:(j + 1) * HEADS0],
                           psum[banks[2 + j % 2]][:, FEAT + HEADS0:ACC_W])

        pipeline(NODE_TILES, [turn, keep, multiply, keep_h])
        sp.dma(lambda e: e.dma_start(node_rows(tab_a0, 0, NODE_TILES), acc[:, :, FEAT:FEAT + HEADS0]),
               store_done, [dve.last()])
        for a in range(0, NODE_TILES, 7):
            sp.dma(lambda e, a=a: e.dma_start(node_rows(tab_h0, a, a + 7), acc[:, a:a + 7, 0:FEAT]),
                   store_done, [dve.last()])
        phase_end()

        score = reg_a[:, :]
        for t in range(STEPS_PAD):
            at = (t % RUN * SEGS + t // RUN) * HEADS0
            gather(score[:, at:at + HEADS0], tab_a0, t, table_done)
        t_scores = tuple(table_done)
        scan_data, scan_fwd = reg_x[:, 0:RUN * P], reg_x[:, RUN * P:2 * RUN * P]
        scan_start, scan_end = reg_acc[:, 0:RUN * P], reg_acc[:, RUN * P:2 * RUN * P]

        bank_free = {}

        def to_scan(out, column, after):
            for j0 in range(0, RUN, 4):
                k = (j0 // 4) % 3
                for j in range(j0, j0 + 4):
                    t = transpose(psum[k][:, (j - j0) * P:(j - j0 + 1) * P], column(j),
                                  list(after) + ([bank_free[k]] if k in bank_free else []))
                bank_free[k] = copy((act, dve)[k % 2], out[:, j0 * P:(j0 + 4) * P], psum[k][:, :], [t])

        def spread(mask, out):
            v = mask.rearrange("p (s j) -> p j s", s=SEGS)
            return copy(dve, out.rearrange("p (j s h) -> p j s h", s=SEGS, h=HEADS0),
                        bcast(v, 3, [P, RUN, SEGS, HEADS0]))

        def run_columns(v):
            return lambda j: v[:, j * P:(j + 1) * P]

        start_spread, end_spread = reg_x[:, 0:RUN * P], reg_x[:, RUN * P:2 * RUN * P]
        t = spread(start_mask, start_spread)
        t2 = spread(end_mask, end_spread)
        to_scan(scan_start, run_columns(start_spread), [t])
        to_scan(scan_end, run_columns(end_spread), [t2])
        t_masks = [act.last(), dve.last()]
        for e in engines[:3]:
            e.wait(*t_masks, pe.last())

        dst_score = reg_b[:, 0:STEPS_PAD * HEADS0].rearrange("p (t h) -> p t h", h=HEADS0)
        hot4 = reg_w[:, 0:2 * 512].rearrange("p (s c e) -> p s c e", s=2, c=4)
        hot4_t = reg_w[:, 1024:2048].rearrange("p (s f) -> p s f", s=2)
        t_hot, t_turned, t_kept, t_exp, t_out = {}, {}, {}, {}, {}

        def expand_hot(g):
            t_hot[g] = tt(hot4[:, g % 2], bcast(iota_row[:, :], 1, [P, 4, P]),
                          bcast(dst_loc[:, 4 * g:4 * g + 4], 2, [P, 4, P]), ALU.is_equal,
                          [t_turned[g - 2]] if g >= 2 else [])

        def expand_turn(g):
            for c in range(4):
                t_turned[g] = transpose(psum[4 + g % 2][:, c * P:(c + 1) * P], hot4[:, g % 2, c, :],
                                        [t_hot[g]] + ([t_kept[g - 2]] if g >= 2 else []))

        def expand_keep(g):
            t_kept[g] = copy(act, hot4_t[:, g % 2, :], psum[4 + g % 2][:, :],
                             [t_turned[g]] + ([t_exp[g - 2]] if g >= 2 else []))

        regs = {}

        def load_tiles(eng, t0, n):
            def make(e):
                if eng not in regs:
                    regs[eng] = [e.alloc_register(f"tile{k}") for k in range(16)]
                e.load(regs[eng][0:n], tile_row[0:1, t0:t0 + n])
            eng.plain(make)

        def tile_value(eng, e, t):
            return e.snap(regs[eng][t % 16], min_val=0, max_val=NODE_TILES - 1)

        def expand_mm(g):
            bank = psum[6 + (g // 4) % 2]
            if g % 4 == 0:
                load_tiles(pe, 4 * g, 16)
            for c in range(4):
                t = 4 * g + c
                t_exp[g] = pe.do(lambda e, t=t, g=g, c=c, bank=bank: e.matmul(
                    bank[:, (t % 16) * HEADS0:(t % 16 + 1) * HEADS0], hot4_t[:, g % 2, c * P:(c + 1) * P],
                    adst[:, bass.DynSlice(tile_value(pe, e, t) * HEADS0, HEADS0)], start=True, stop=True),
                    [t_kept[g]] + ([t_out[g // 4 - 2]] if g // 4 >= 2 else []))
            if g % 4 == 3:
                t_out[g // 4] = copy(act, dst_score[:, 4 * g - 12:4 * g + 4, :].rearrange("p t h -> p (t h)"),
                                     bank[:, 0:16 * HEADS0], [t_exp[g]])

        pipeline(STEPS_PAD // 4, [expand_hot, expand_turn, expand_keep, expand_mm])

        score_by_run = score.rearrange("p (j s h) -> p j s h", s=SEGS, h=HEADS0)
        t = tt(score_by_run, score_by_run, bcast(cap.rearrange("p (s j) -> p j s", s=SEGS), 3,
                                                 [P, RUN, SEGS, HEADS0]), ALU.min, [t_scores])
        to_scan(scan_data, run_columns(score), [t])
        t_data = [act.last(), dve.last()]

        def scan(out, mask, data, initial, after):
            return dve.do(lambda e: e.tensor_tensor_scan(out, mask, data, initial, ALU.add, ALU.max), after)

        tails = small[:, 0:4]
        t = scan(scan_fwd, scan_start, scan_data, LOW, t_data)
        t = copy(dve, tails[:, 0:1], scan_fwd[:, RUN * P - 1:RUN * P], [t])
        dve.do(lambda e: e.tensor_reduce(tails[:, 1:2], scan_start, AXX, ALU.min))
        t = scan(scan_fwd[:, ::-1], scan_end[:, ::-1], scan_data[:, ::-1], LOW, [t])
        copy(dve, tails[:, 2:3], scan_fwd[:, 0:1], [t])
        t = dve.do(lambda e: e.tensor_reduce(tails[:, 3:4], scan_end, AXX, ALU.min))
        for k in range(4):
            t_row = transpose(psum[0][0:1, k * P:(k + 1) * P], tails[:, k:k + 1], [t, bank_free[0]])
        row = reg_w[0:1, 0:4 * P].rearrange("p (k h s) -> p k h s", k=4, h=HEADS0)
        t = copy(dve, row, psum[0][0:1, :].rearrange("p (k s h) -> p k h s", k=4, h=HEADS0), [t_row])
        t = dve.do(lambda e: e.memset(row[:, 1, :, 0:1], LOW), [t])
        t = dve.do(lambda e: e.memset(row[:, 3, :, SEGS - 1:SEGS], LOW), [t])
        state = reg_w[0:1, 512:512 + 2 * P]
        flat = reg_w[0:1, 0:4 * P]
        scan(state[:, 0:P], flat[:, P:2 * P], flat[:, 0:P], LOW, [t])
        t = scan(state[:, P:2 * P][:, ::-1], flat[:, 3 * P:4 * P][:, ::-1], flat[:, 2 * P:3 * P][:, ::-1], LOW, [])
        carry = reg_w[0:1, 1024:1024 + 2 * P].rearrange("p (k s h) -> p k h s", k=2, h=HEADS0)
        st = state.rearrange("p (k h s) -> p k h s", k=2, h=HEADS0)
        t0 = dve.do(lambda e: e.memset(reg_w[0:1, 1024:1024 + 2 * P], LOW))
        copy(dve, carry[:, 0, :, 1:SEGS], st[:, 0, :, 0:SEGS - 1], [t, t0])
        t = copy(dve, carry[:, 1, :, 0:SEGS - 1], st[:, 1, :, 1:SEGS])
        for k in range(2):
            t_col = transpose(psum[1][:, k:k + 1], reg_w[0:1, 1024 + k * P:1024 + (k + 1) * P], [t, bank_free[1]])
        carries = small[:, 8:10]
        t = copy(dve, carries, psum[1][:, 0:2], [t_col])
        scan(scan_fwd, scan_start, scan_data, carries[:, 0:1], [t])
        t = scan(scan_data[:, ::-1], scan_end[:, ::-1], scan_data[:, ::-1], carries[:, 1:2], [dve.last()])
        t_max = tt(scan_fwd, scan_fwd, scan_data, ALU.max, [t])
        largest = reg_acc[:, 0:STEPS_PAD * HEADS0]
        for j in range(RUN):
            k = j % 3
            t = transpose(psum[k][:, 0:P], scan_fwd[:, j * P:(j + 1) * P], [t_max, bank_free[k]])
            bank_free[k] = copy((act, dve)[j % 2], largest[:, j * P:(j + 1) * P], psum[k][:, 0:P], [t])
        for e in engines:
            e.wait(act.last(), dve.last(), pe.last())

        def leaky(v, after):
            return stt(v, v, 0.2, v, ALU.mult, ALU.max, after)

        def in_steps(v):
            return v.rearrange("p (j s h) -> p s j h", s=SEGS, h=HEADS0)

        of_dst = dst_score.rearrange("p (s j) h -> p s j h", s=SEGS)
        t_s = leaky(score, [tt(in_steps(score), in_steps(score), of_dst, ALU.add)])
        t_m = leaky(largest, [tt(in_steps(largest), in_steps(largest), of_dst, ALU.add)])
        t = tt(score, score, largest, ALU.subtract, [t_s, t_m])
        weight0 = reg_b[:, :].rearrange("p (t h) -> p t h", h=HEADS0 + 1)
        activate(weight0[:, :, 0:HEADS0].rearrange("p (s j) h -> p s j h", s=SEGS), in_steps(score), ACT.Exp, [t])
        dve.do(lambda e: e.memset(weight0[:, :, HEADS0:HEADS0 + 1], 1.0), [t])
        dve.do(lambda e: e.memset(reg_acc[:, :], 0.0))
        t = load_x([dve.last()])
        phase_end()

        n_hot, n_bank, lag = 4, 6, 2
        rows = reg_a[:, 0:n_gather * FEAT].rearrange("p (s f) -> p s f", f=FEAT)
        hots = reg_a[:, n_gather * FEAT:n_gather * FEAT + n_hot * P].rearrange("p (s f) -> p s f", f=P)
        rest = reg_a[:, n_gather * FEAT + n_hot * P:]
        reverse = rest[:, 0:4 * OUT3].rearrange("p (s f) -> p s f", s=4)
        message = rest[:, 4 * OUT3:8 * OUT3].rearrange("p (s f) -> p s f", s=4)
        scaled = rest[:, 8 * OUT3:8 * OUT3 + 4 * FEAT].rearrange("p (s f) -> p s f", s=4)

        def edge_pass(table, kind, extra=0, weights=None):
            width = FEAT + extra
            t_got, t_hot, t_rhs, t_mm, t_add, t_rev = {}, {}, {}, {}, {}, {}
            row_w = table.shape[1]

            def fetch(i):
                free = {"mix": t_rhs}.get(kind, t_mm).get(i - n_gather)
                t_got[i] = gather(rows[:, i % n_gather, 0:row_w], table, i, gather_done[i % n_gather],
                                  [free] if free else [])

            def prepare(i):
                hot, row = hots[:, i % n_hot, :], rows[:, i % n_gather, :]
                free = [t_mm[i - n_hot]] if i >= n_hot else []
                if kind == "weighted":
                    t_hot[i] = ts(hot, iota_row[:, :], dst_loc[:, i:i + 1], edge_w[:, i:i + 1], ALU.is_equal,
                                  ALU.mult, after=free)
                elif kind != "mix":
                    t_hot[i] = ts(hot, iota_row[:, :], dst_loc[:, i:i + 1], None, ALU.is_equal, after=free)
                if kind == "heads":
                    v = row.rearrange("p (h d) -> p h d", h=HEADS0)
                    t_rhs[i] = tt(v, v, bcast(weights[:, i, 0:HEADS0], 2, [P, HEADS0, HEAD0_DIM]), ALU.mult,
                                  [t_got[i]])
                elif kind == "mix":
                    s = i % 4
                    t_rev[i] = act.do(lambda e: e.mul(reverse[:, s, :], row[:, OUT3:2 * OUT3], attr1[:, i:i + 1]),
                                      [t_got[i]] + ([t_mm[i - 4]] if i >= 4 else []))
                    t_msg = stt(message[:, s, :], row[:, 0:OUT3], attr0[:, i:i + 1], reverse[:, s, :], ALU.mult,
                                ALU.add, [t_rev[i]])
                    t_hot[i] = ts(hot, iota_row[:, :], dst_loc[:, i:i + 1], None, ALU.is_equal, after=free)
                    t_rhs[i] = tt(scaled[:, s, :].rearrange("p (h d) -> p h d", h=HEADS3),
                                  bcast(message[:, s, :], 1, [P, HEADS3, OUT3]),
                                  bcast(weights[:, i, :], 2, [P, HEADS3, OUT3]), ALU.mult, [t_msg])

            def product(i):
                bank = psum[i % n_bank]
                hot = hots[:, i % n_hot, :]
                rhs = scaled[:, i % 4, :] if kind == "mix" else rows[:, i % n_gather, :]
                after = [t_hot[i], t_rhs.get(i, t_got[i])] + ([t_add[i - n_bank]] if i >= n_bank else [])
                t_mm[i] = mm(bank[:, 0:FEAT], hot, rhs, after=after)
                if extra:
                    t_mm[i] = mm(bank[:, FEAT:width], hot, weights[:, i, 0:extra])

            def add(i):
                if i % 16 == 0:
                    load_tiles(dve, i, min(16, STEPS - i))

                def make(e):
                    a = reg_acc[:, bass.DynSlice(tile_value(dve, e, i) * ACC_W, width)]
                    return e.tensor_tensor(a, a, psum[i % n_bank][:, 0:width], ALU.add)
                t_add[i] = dve.do(make, [t_mm[i]] + ([t_add[i - 1]] if i else []))

            for i in range(STEPS + lag):
                if i < STEPS:
                    fetch(i)
                    prepare(i)
                    product(i)
                if i >= lag:
                    add(i - lag)
            phase_end()

        group = 7
        groups = NODE_TILES // group
        scratch = reg_b[:, 0:group * FEAT].rearrange("p (t f) -> p t f", f=FEAT)
        stats = reg_b[:, 4096:4096 + NODE_TILES * 6].rearrange("p (t k) -> p t k", k=6)
        moments = reg_b[:, 4500:4500 + NODE_TILES * 2].rearrange("p (t k) -> p t k", k=2)
        rstd = reg_b[:, 4700:4700 + NODE_TILES]
        shift = reg_b[:, 4800:4800 + NODE_TILES]
        recip = reg_b[:, 5000:5000 + NODE_TILES * HEADS0].rearrange("p (t h) -> p t h", h=HEADS0)

        def eps_rsqrt(out, a, eps, after):
            t = ts(out, a, eps, None, ALU.add, after=after)
            t = activate(out, out, ACT.Sqrt, [t])
            return dve.do(lambda e: e.reciprocal(out, out), [t])

        def normalise(src, out, after=()):
            for j in range(NODE_TILES):
                t = dve.do(lambda e, j=j: e.bn_stats(stats[:, j, :], src(j)), after)
            for j in range(NODE_TILES):
                t = dve.do(lambda e, j=j: e.bn_aggr(moments[:, j, :], stats[:, j, :]), [t] if not j else [])
            t = eps_rsqrt(rstd, moments[:, :, 1], LN_EPS, [t])
            t = stt(shift, moments[:, :, 0], -1.0, rstd, ALU.mult, ALU.mult, [t])
            for j in range(NODE_TILES):
                t = activate(out(j), src(j), ACT.Identity, [t], scale=rstd[:, j:j + 1], bias=shift[:, j:j + 1])
            return t

        def load_vectors(names, at):
            out = []
            for name in names:
                n = io[name].shape[-1]
                load(reg_w[:, at:at + n], io[name].partition_broadcast(P))
                out.append(reg_w[:, at:at + n])
                at += n
            return out

        def heads_mean(n_heads, eps, out_dim):
            r = recip[:, :, 0:n_heads]
            t = ts(r, acc[:, :, FEAT:FEAT + n_heads], eps, None, ALU.add)
            t = dve.do(lambda e: e.reciprocal(r, r), [t])
            for j in range(NODE_TILES):
                v = acc[:, j, 0:FEAT].rearrange("p (h d) -> p h d", h=n_heads)
                t_last = tt(v, v, bcast(r[:, j, :], 2, [P, n_heads, out_dim]), ALU.mult, [t])
            return t_last

        def store_table(table, view, after):
            for a in range(0, NODE_TILES, group):
                sp.dma(lambda e, a=a: e.dma_start(node_rows(table, a, a + group), view[:, a:a + group, :]),
                       store_done, after)

        edge_pass(tab_h0, "heads", HEADS0 + 1, weight0)
        (bias0,) = load_vectors(["bias0"], 0)
        t = copy(dve, dinv[:, :], acc[:, :, FEAT + HEADS0])
        eps_rsqrt(dinv[:, :], dinv[:, :], 1.0, [t])
        t = heads_mean(HEADS0, 1e-16, HEAD0_DIM)
        for a in range(0, NODE_TILES, group):
            v, x = acc[:, a:a + group, 0:FEAT], x_sb[:, a:a + group, :]
            t = tt(v, v, bcast(bias0, 1, [P, group, FEAT]), ALU.add, [t, tuple(load_done)])
            t = stt(x, v, 0.0, x, ALU.max, ALU.add, [t])
        t = normalise(lambda j: x_sb[:, j, :], lambda j: x_sb[:, j, :], [t])
        for j in range(NODE_TILES):
            t = act.do(lambda e, j=j: e.mul(acc[:, j, 0:FEAT], x_sb[:, j, :], dinv[:, j:j + 1]), [t])
        store_table(tab_x1, acc[:, :, 0:FEAT], [t])
        phase_end()

        edge_pass(tab_x1, "plain")
        w1 = reg_w[:, 0:2 * HIDDEN].rearrange("p (k f) -> p k f", k=2)
        w2 = reg_w[:, 2 * HIDDEN:4 * HIDDEN].rearrange("p (k f) -> p k f", k=4)
        load(w1, io["w1"].rearrange("(k p) f -> p k f", p=P))
        load(w2, io["w2"].rearrange("(k p) f -> p k f", p=P))
        bias1, gamma1, beta1 = load_vectors(["b1", "gamma1", "beta1"], 4 * HIDDEN)
        t_loads = tuple(load_done)
        turned = reg_a[:, 0:4 * P]
        turn, keep, multiply, t_mm, used, banks = matmul_stages(
            lambda j: acc[:, j, 0:FEAT], 2, w1, HIDDEN, turned, lambda j: [t_loads])
        hid = reg_a[:, 1024:1024 + 4 * HIDDEN].rearrange("p (s f) -> p s f", s=4)
        t_stat, t_norm, t_hid = {}, {}, {}

        def hidden_in(j):
            h = hid[:, j % 4, :]
            used[j] = t = stt(h, psum[banks[2 + j % 2]][:, :], dinv[:, j:j + 1], bias1, ALU.mult, ALU.add,
                              [t_mm[j], t_loads] + ([t_turn2[j - 4]] if j >= 4 else []))
            t = dve.do(lambda e: e.bn_stats(stats[:, j, :], h), [t])
            t = dve.do(lambda e: e.bn_aggr(moments[:, j, :], stats[:, j, :]), [t])
            t = ts(rstd[:, j:j + 1], moments[:, j, 1:2], LN_EPS, None, ALU.add, after=[t])
            t_stat[j] = activate(rstd[:, j:j + 1], rstd[:, j:j + 1], ACT.Sqrt, [t])

        def hidden_norm(j):
            h = hid[:, j % 4, :]
            t = dve.do(lambda e: e.reciprocal(rstd[:, j:j + 1], rstd[:, j:j + 1]), [t_stat[j]])
            t = ts(h, h, moments[:, j, 0:1], rstd[:, j:j + 1], ALU.subtract, ALU.mult, after=[t])
            t = tt(h, h, gamma1, ALU.mult, [t])
            t_norm[j] = tt(h, h, beta1, ALU.add, [t])
            t_hid[j] = activate(h, h, ACT.Relu, [t_norm[j]])

        turned2 = reg_a[:, 3072:3072 + 8 * P]
        turn2, keep2, multiply2, t_mm2, used2, banks2 = matmul_stages(
            lambda j: hid[:, j % 4, :], 4, w2, FEAT, turned2, lambda j: [t_hid[j]], banks=(4, 5, 6, 7))
        t_turn2 = {}

        def turn2_noted(j):
            turn2(j)
            t_turn2[j] = pe.last()

        def hidden_out(j):
            used2[j] = act.do(lambda e: e.mul(acc[:, j, 0:FEAT], psum[banks2[2 + j % 2]][:, 0:FEAT], dinv[:, j:j + 1]),
                              [t_mm2[j]])

        pipeline(NODE_TILES, [turn, keep, multiply, hidden_in, hidden_norm, turn2_noted, keep2, multiply2, hidden_out])
        store_table(tab_h2, acc[:, :, 0:FEAT], [act.last()])
        phase_end()

        edge_pass(tab_h2, "plain")
        bias2, gamma2, beta2 = load_vectors(["b2", "gamma2", "beta2"], 0)
        t = dve.last()
        for j in range(NODE_TILES):
            v = acc[:, j, 0:FEAT]
            t = stt(v, v, dinv[:, j:j + 1], bias2, ALU.mult, ALU.add, [tuple(load_done)])
        t = normalise(lambda j: acc[:, j, 0:FEAT], lambda j: acc[:, j, 0:FEAT], [t])
        for a in range(0, NODE_TILES, group):
            v, x = acc[:, a:a + group, 0:FEAT], x_sb[:, a:a + group, :]
            t = tt(v, v, bcast(gamma2, 1, [P, group, FEAT]), ALU.mult, [t])
            t = tt(v, v, bcast(beta2, 1, [P, group, FEAT]), ALU.add, [t])
            t = stt(x, v, 0.0, x, ALU.max, ALU.add, [t])
        t = normalise(lambda j: x_sb[:, j, :], lambda j: x_sb[:, j, :], [t])
        store_table(tab_x2, x_sb, [t])
        dve.do(lambda e: e.memset(reg_acc[:, :], 0.0))
        phase_end()

        edge_pass(tab_x2, "weighted")
        wl2 = reg_w[:, 0:2 * FEAT].rearrange("p (k f) -> p k f", k=2)
        load(wl2, io["w_l2"].rearrange("(k p) f -> p k f", p=P))
        (bias_l2,) = load_vectors(["b_l2"], 2 * FEAT)
        t_loads = tuple(load_done)
        turn, keep, multiply, t_mm, used, banks = matmul_stages(
            lambda j: acc[:, j, 0:FEAT], 2, wl2, FEAT, turned, lambda j: [t_loads])
        t_bias = {}

        def l2_out(j):
            v = acc[:, j, 0:FEAT]
            used[j] = t = tt(v, psum[banks[2 + j % 2]][:, 0:FEAT], bias_l2, ALU.add, [t_mm[j], t_loads])
            stt(x_sb[:, j, :], v, 0.0, x_sb[:, j, :], ALU.max, ALU.add, [t])

        pipeline(NODE_TILES, [turn, keep, multiply, l2_out])
        normalise(lambda j: x_sb[:, j, :], lambda j: x_sb[:, j, :], [dve.last()])
        phase_end()

        w3_w = 2 * OUT3 + 2 * HEADS3
        w3 = reg_w[:, 0:2 * w3_w].rearrange("p (k f) -> p k f", k=2)
        raw = reg_w[0:OUT3, 512:512 + 2 * FEAT].rearrange("p (d f) -> p d f", d=2)
        attn_row = reg_w[0:HEADS3, 1024:1024 + OUT3]
        turner = reg_w[0:OUT3, 1100:1100 + OUT3 + HEADS3]
        load(raw[:, 0, :], io["w_fwd"])
        load(raw[:, 1, :], io["w_rev"])
        t = load(attn_row, io["attn"])
        t = transpose(psum[0][0:OUT3, 0:HEADS3], attn_row, [t])
        copy(dve, turner[:, OUT3:OUT3 + HEADS3], psum[0][0:OUT3, 0:HEADS3], [t])
        t = copy(dve, turner[:, 0:OUT3], ident[0:OUT3, 0:OUT3])
        for d in range(2):
            for k in range(2):
                bank = psum[1 + 2 * d + k]
                t_w = mm(bank[:, 0:OUT3 + HEADS3], raw[:, d, k * P:(k + 1) * P], turner, after=[t])
                copy(dve, w3[:, k, d * OUT3:(d + 1) * OUT3], bank[:, 0:OUT3], [t_w])
                copy(dve, w3[:, k, 2 * OUT3 + d * HEADS3:2 * OUT3 + (d + 1) * HEADS3], bank[:, OUT3:OUT3 + HEADS3])
        t_w3 = dve.last()
        for e in (pe, act):
            e.wait(t_w3)
        turn, keep, multiply, t_mm, used, banks = matmul_stages(
            lambda j: x_sb[:, j, :], 2, w3, w3_w, turned, lambda j: [])

        def l3_keep(j):
            used[j] = copy(dve, acc[:, j, 0:w3_w], psum[banks[2 + j % 2]][:, 0:w3_w], [t_mm[j]])

        pipeline(NODE_TILES, [turn, keep, multiply, l3_keep])
        store_table(tab_h3, acc[:, :, 0:2 * OUT3], [dve.last()])
        sp.dma(lambda e: e.dma_start(node_rows(tab_a3, 0, NODE_TILES), acc[:, :, 2 * OUT3:w3_w]),
               store_done, [dve.last()])
        phase_end()

        score = score.rearrange("p (t h) -> p t h", h=HEADS0)
        for t in range(STEPS_PAD):
            gather(score[:, t, :], tab_a3, t, table_done)
        dve.do(lambda e: e.memset(reg_acc[:, :], 0.0))
        t = tuple(table_done)
        s4 = [P, STEPS_PAD, HEADS3]
        tt(score[:, :, 0:HEADS3], score[:, :, 0:HEADS3], bcast(attr0[:, :], 2, s4), ALU.mult, [t])
        t = tt(score[:, :, HEADS3:], score[:, :, HEADS3:], bcast(attr1[:, :], 2, s4), ALU.mult)
        weight3 = reg_b[:, 0:STEPS_PAD * HEADS3].rearrange("p (t h) -> p t h", h=HEADS3)
        t = leaky(weight3, [tt(weight3, score[:, :, 0:HEADS3], score[:, :, HEADS3:], ALU.add, [t])])
        top = small[:, 16:16 + HEADS3]
        top_all = small[:, 24:24 + HEADS3]
        t = dve.do(lambda e: e.tensor_reduce(top, weight3.rearrange("p t h -> p h t"), AXX, ALU.max), [t])
        t = pool.do(lambda e: e.partition_all_reduce(top_all, top, P, bass.bass_isa.ReduceOp.max), [t])
        t = tt(weight3, weight3, bcast(top_all, 1, s4), ALU.subtract, [t])
        activate(weight3, weight3, ACT.Exp, [t])
        phase_end()

        edge_pass(tab_h3, "mix", HEADS3, weight3)
        t = heads_mean(HEADS3, 1e-10, OUT3)
        for a in range(0, NODE_TILES, group):
            v, x = acc[:, a:a + group, 0:FEAT], x_sb[:, a:a + group, :]
            t = tt(x, v, x, ALU.add, [t])
        t = normalise(lambda j: x_sb[:, j, :], lambda j: x_sb[:, j, :], [t])
        out_rows = io["out"][0:FULL_TILES * P, :].rearrange("(t p) f -> p t f", p=P)
        out_done = [sem("s_out"), 0]
        sp.dma(lambda e: e.dma_start(out_rows, x_sb[:, 0:FULL_TILES, :]), out_done, [t])
        sp.dma(lambda e: e.dma_start(io["out"][FULL_TILES * P:NODES, :], x_sb[0:TAIL_ROWS, FULL_TILES, :]),
               out_done, [t])
        sp.wait(tuple(out_done), tuple(store_done))

        block = ctx.enter_context(nc.Block())

        @block.tensor
        def _(e):
            pe.replay(e)

        @block.vector
        def _(e):
            dve.replay(e)

        @block.scalar
        def _(e):
            act.replay(e)

        @block.gpsimd
        def _(e):
            pool.replay(e)

        @block.sync
        def _(e):
            sp.replay(e)


def kernel(x, src, dst, edge_attr_2, edge_weight, L0_gnn_W, L0_gnn_att_src, L0_gnn_att_dst, L0_gnn_bias, L1_gnn_W1,
           L1_gnn_b1, L1_gnn_gamma1, L1_gnn_beta1, L1_gnn_W2, L1_gnn_b2, L1_gnn_gamma2, L1_gnn_beta2, L2_gnn_W,
           L2_gnn_b, L3_gnn_W_forward, L3_gnn_W_reverse, L3_gnn_attn_forward):
    import concourse.bacc as bacc
    from concourse.bass_utils import run_bass_kernel_spmd

    fill = EDGES_PAD - EDGES
    src, dst = np.asarray(src), np.asarray(dst)
    attr, weight = np.asarray(edge_attr_2), np.asarray(edge_weight)
    none = np.full(1, -1, dst.dtype)
    dst_pad = np.concatenate([dst, np.full(fill, JUNK_NODE, dst.dtype)])
    edge_ints = np.concatenate([v.reshape(CHUNKS, P) for v in (
        np.concatenate([src, src[-fill:]]), dst_pad, np.concatenate([none, dst_pad[:-1]]),
        np.concatenate([dst_pad[1:], none]))], axis=1)
    edge_floats = np.concatenate([np.concatenate([attr, attr[-fill:]]).reshape(CHUNKS, 2 * P),
                                  np.concatenate([weight, weight[-fill:]]).reshape(CHUNKS, P)], axis=1)
    ins = {
        "x": x, "edge_ints": edge_ints, "edge_floats": edge_floats,
        "w0": np.asarray(L0_gnn_W).reshape(FEAT, FEAT), "att_src": np.asarray(L0_gnn_att_src).reshape(FEAT),
        "att_dst": np.asarray(L0_gnn_att_dst).reshape(FEAT), "bias0": L0_gnn_bias,
        "w1": L1_gnn_W1, "b1": L1_gnn_b1, "gamma1": L1_gnn_gamma1, "beta1": L1_gnn_beta1,
        "w2": L1_gnn_W2, "b2": L1_gnn_b2, "gamma2": L1_gnn_gamma2, "beta2": L1_gnn_beta2,
        "w_l2": L2_gnn_W, "b_l2": L2_gnn_b, "w_fwd": L3_gnn_W_forward, "w_rev": L3_gnn_W_reverse,
        "attn": np.asarray(L3_gnn_attn_forward).reshape(HEADS3, OUT3),
    }
    nc = bacc.Bacc("TRN2", target_bir_lowering=False, num_devices=1)
    arrays, io = {}, {}
    for name, a in ins.items():
        a = np.ascontiguousarray(a)
        arrays[f"in_{name}"] = a
        io[name] = nc.dram_tensor(f"in_{name}", a.shape, mybir.dt.from_np(a.dtype), kind="ExternalInput").ap()
    io["out"] = nc.dram_tensor("out_0", (NODES, FEAT), F32, kind="ExternalOutput").ap()
    build(nc, io)
    r = run_bass_kernel_spmd(nc, [arrays], core_ids=[0])
    return r.results[0]["out_0"]
```

```python
from contextlib import ExitStack

import numpy as np

import concourse.bass as bass
from concourse import mybir

F32 = mybir.dt.float32
I32 = mybir.dt.int32
ALU = mybir.AluOpType
ACT = mybir.ActivationFunctionType
AXX = mybir.AxisListType.X

P = 128
NODES = 6250
EDGES = 100000
FEAT = 256
NODE_TILES = -(-NODES // P)
NODES_PAD = NODE_TILES * P
FULL_TILES = NODES // P
TAIL_ROWS = NODES - FULL_TILES * P
CHUNKS = -(-EDGES // P)
EDGES_PAD = CHUNKS * P
STEPS = CHUNKS + NODE_TILES - 1
GROUP = 16
GROUPS = -(-STEPS // GROUP)
STEPS_PAD = GROUPS * GROUP
STEP_BLOCKS = -(-STEPS_PAD // P)
HEADS0 = 8
HEAD0_DIM = FEAT // HEADS0
HEADS3 = 4
OUT3 = 64
HIDDEN = 512
ROW3 = 2 * OUT3 + 2 * HEADS3
ROW0 = FEAT + HEADS0
ACC_W = FEAT + 2 * HEADS0
LOW = -1.0e38
LN_EPS = 1e-5
JUNK_NODE = NODES_PAD - 1


class Engine:

    def __init__(self, sem):
        self.sem, self.count, self.queue, self.seen = sem, 0, [], {}

    def wait(self, *tokens):
        for sem, value in tokens:
            if self.seen.get(id(sem), 0) < value:
                self.seen[id(sem)] = value
                self.queue.append(lambda e, s=sem, v=value: e.wait_ge(s, v))

    def do(self, make, after=()):
        self.wait(*after)
        self.count += 1
        self.queue.append(lambda e: make(e).then_inc(self.sem, 1))
        return (self.sem, self.count)

    def dma(self, make, done, after=()):
        self.wait(*after)
        done[1] += 16
        self.queue.append(lambda e: make(e).then_inc(done[0], 16))
        return (done[0], done[1])

    def plain(self, make):
        self.queue.append(make)

    def last(self):
        return (self.sem, self.count)

    def replay(self, e):
        for step in self.queue:
            step(e)


def pipeline(n, stages):
    for i in range(n + len(stages) - 1):
        for k in range(len(stages) - 1, -1, -1):
            if 0 <= i - k < n:
                stages[k](i - k)


def build(nc, io):
    ctx = ExitStack()
    with ctx:
        def sb(name, width, dt=F32, rows=P):
            return ctx.enter_context(nc.sbuf_tensor(name, [rows, width], dt))

        def sem(name):
            return ctx.enter_context(nc.semaphore(name))

        def dram(name, shape, dt=F32):
            return nc.dram_tensor(name, shape, dt, kind="Internal").ap()

        reg_x = sb("reg_x", max(NODE_TILES * FEAT, 3 * GROUP * (ROW0 + 1)))
        reg_acc = sb("reg_acc", NODE_TILES * ACC_W)
        reg_a = sb("reg_a", 3 * GROUP * ROW3)
        reg_b = sb("reg_b", 7488)
        reg_w = sb("reg_w", 7 * HIDDEN)
        src_idx = sb("src_idx", STEPS_PAD, I32)
        dst_loc = sb("dst_loc", STEPS_PAD)
        edge_w = sb("edge_w", STEPS_PAD)
        attr0 = sb("attr0", STEPS_PAD)
        attr1 = sb("attr1", STEPS_PAD)
        cap = sb("cap", STEPS_PAD)[:, :]
        tile_row = sb("tile_row", STEPS_PAD, I32, rows=1)
        group_row = sb("group_row", NODE_TILES, I32, rows=1)
        ident = sb("ident", P)
        iota_row = sb("iota_row", P)
        adst = sb("adst", NODE_TILES * HEADS0)
        dinv = sb("dinv", NODE_TILES)
        small = sb("small", 512)
        psum = [ctx.enter_context(nc.psum_tensor(f"bank{k}", [P, 512], F32)) for k in range(8)]

        tab_h0 = dram("tab_h0", [NODES_PAD, ROW0])
        tab_x1 = dram("tab_x1", [NODES_PAD, FEAT])
        tab_h2 = dram("tab_h2", [NODES_PAD, FEAT])
        tab_x2 = dram("tab_x2", [NODES_PAD, FEAT])
        tab_h3 = dram("tab_h3", [NODES_PAD, ROW3])
        tile_dram = dram("tile_dram", [STEP_BLOCKS * P, 1], I32)
        group_dram = dram("group_dram", [NODE_TILES, 1], I32)

        pe, dve, act, pool, sp = (Engine(sem(f"s_{n}")) for n in ("pe", "dve", "act", "pool", "sp"))
        engines = (pe, dve, act, pool, sp)
        load_done = [sem("s_load"), 0]
        load2_done = [sem("s_load2"), 0]
        store_done = [sem("s_store"), 0]
        table_done = [sem("s_table"), 0]
        n_gather = 12
        gather_done = [[sem(f"s_gather{k}"), 0] for k in range(n_gather)]
        group_done = [[sem(f"s_group{k}"), 0] for k in range(3)]
        counters = [load_done, load2_done, store_done, table_done] + gather_done + group_done

        def phase_end():
            tokens = [e.last() for e in engines] + [tuple(c) for c in counters]
            for e in engines:
                e.wait(*tokens)

        def tt(out, a, b, op, after=(), eng=None):
            return (eng or dve).do(lambda e: e.tensor_tensor(out, a, b, op), after)

        def ts(out, a, s1, s2, op0, op1=None, after=()):
            if op1 is None:
                return dve.do(lambda e: e.tensor_scalar(out, a, s1, None, op0), after)
            return dve.do(lambda e: e.tensor_scalar(out, a, s1, s2, op0, op1), after)

        def stt(out, a, s, b, op0, op1, after=()):
            return dve.do(lambda e: e.scalar_tensor_tensor(out=out, in0=a, scalar=s, in1=b, op0=op0, op1=op1), after)

        def copy(eng, out, a, after=()):
            if eng is act:
                return act.do(lambda e: e.copy(out, a), after)
            return eng.do(lambda e: e.tensor_copy(out, a), after)

        def activate(out, a, fn, after=(), **kw):
            return act.do(lambda e: e.activation(out, a, fn, **kw), after)

        def mm(out, lhs_t, rhs, start=True, stop=True, after=()):
            return pe.do(lambda e: e.matmul(out, lhs_t, rhs, start=start, stop=stop), after)

        def transpose(out, a, after=()):
            n = a.shape[0]
            return pe.do(lambda e: e.transpose(out, a, ident[0:n, 0:n]), after)

        def load(out, a, after=()):
            return sp.dma(lambda e: e.dma_start(out, a), load_done, after)

        def gather(out, table, t, done, after=()):
            return pool.dma(lambda e: e.indirect_dma_start(
                out, None, table, bass.IndirectOffsetOnAxis(ap=src_idx[:, t:t + 1], axis=0)), done, after)

        def node_rows(table, a, b):
            return table.rearrange("(t p) f -> p t f", p=P)[:, a:b, :]

        def bcast(ap, axis, shape):
            return ap.unsqueeze(axis).to_broadcast(shape)

        x_sb = reg_x[:, 0:NODE_TILES * FEAT].rearrange("p (t f) -> p t f", f=FEAT)
        acc = reg_acc[:, :].rearrange("p (t f) -> p t f", f=ACC_W)

        small_i = small[:, 0:P].bitcast(I32)
        t_iota = pool.do(lambda e: e.iota(small_i, pattern=[[1, P]], base=0, channel_multiplier=0))
        t_part = pool.do(lambda e: e.iota(small[:, P:P + 1].bitcast(I32), pattern=[[0, 1]], base=0,
                                          channel_multiplier=1))
        step_i = small[:, 144:144 + STEP_BLOCKS].bitcast(I32)
        t_step = pool.do(lambda e: e.iota(step_i, pattern=[[P, STEP_BLOCKS]], base=0, channel_multiplier=1))
        chunk_i = reg_a[0:1, 0:CHUNKS].bitcast(I32)
        t_chunk = pool.do(lambda e: e.iota(chunk_i, pattern=[[1, CHUNKS]], base=1, channel_multiplier=0))
        copy(dve, iota_row[:, :], small_i, [t_iota])
        part = small[:, 130:131]
        t = copy(dve, part, small[:, P:P + 1].bitcast(I32), [t_part])
        ts(ident[:, :], iota_row[:, :], part, None, ALU.is_equal, after=[t])
        step_no = small[:, 160:160 + STEP_BLOCKS]
        copy(dve, step_no, step_i, [t_step])
        ones_row = small[0:1, 200:200 + P]
        dve.do(lambda e: e.memset(ones_row, 1.0))

        last_dst = reg_a[0:1, 800:800 + CHUNKS].bitcast(I32)
        ends = io["edge_ints"][:, 2 * P - 1:2 * P].rearrange("c k -> k c")
        t = sp.dma(lambda e: e.dma_start(last_dst, ends, allow_slow_non_contiguous=True), load_done)
        last_tile = reg_a[0:1, 1600:1600 + CHUNKS].bitcast(I32)
        t = dve.do(lambda e: e.tensor_scalar(last_tile, last_dst, 7, None, ALU.arith_shift_right), [t])
        bound = reg_a[0:1, 2400:2400 + CHUNKS]
        t = tt(bound, last_tile, chunk_i, ALU.add, [t, t_chunk])
        half = CHUNKS // 2
        mm(psum[0][:, 0:half], ones_row, bound[:, 0:half], after=[t])
        t = mm(psum[1][:, 0:CHUNKS - half], ones_row, bound[:, half:CHUNKS])
        bounds = reg_a[:, 3200:3200 + CHUNKS]
        copy(dve, bounds[:, 0:half], psum[0][:, 0:half], [t])
        t = copy(dve, bounds[:, half:CHUNKS], psum[1][:, 0:CHUNKS - half])
        chunk_of = small[:, 170:170 + STEP_BLOCKS]
        hits = reg_a[:, 4000:4000 + CHUNKS]
        for b in range(STEP_BLOCKS):
            t = dve.do(lambda e, b=b: e.tensor_scalar(hits, bounds, step_no[:, b:b + 1], 0.0, ALU.is_le, ALU.add,
                                                      accum_out=chunk_of[:, b:b + 1]), [t])
        t = ts(chunk_of, chunk_of, float(CHUNKS - 1), None, ALU.min, after=[t])
        tile_of = small[:, 180:180 + STEP_BLOCKS]
        chunk_idx = small[:, 190:190 + STEP_BLOCKS].bitcast(I32)
        t_idx = copy(dve, chunk_idx, chunk_of, [t])
        t = tt(tile_of, step_no, chunk_of, ALU.subtract, [t])
        first_node = small[:, 330:330 + STEP_BLOCKS]
        t_first = ts(first_node, tile_of, float(P), None, ALU.mult, after=[t])
        tile_i = small[:, 340:340 + STEP_BLOCKS].bitcast(I32)
        t = ts(tile_i, tile_of, float(NODE_TILES - 1), None, ALU.min, after=[t])
        t = sp.dma(lambda e: e.dma_start(tile_dram.rearrange("(b p) k -> p (b k)", p=P), tile_i,
                                              allow_slow_non_contiguous=True), store_done, [t])
        t = sp.dma(lambda e: e.dma_start(tile_row[:, :], tile_dram[0:STEPS_PAD, :].rearrange("s k -> k s")),
                   load2_done, [t])

        tile_f = reg_a[0:1, 800:800 + STEPS_PAD]
        t = copy(dve, tile_f, tile_row[:, :], [t])
        half = STEPS_PAD // 2
        for k in range(2):
            t_b = mm(psum[2 + k][:, 0:half], ones_row, tile_f[:, k * half:(k + 1) * half], after=[t])
        tiles_all = reg_a[:, 1700:1700 + STEPS_PAD]
        for k in range(2):
            t = copy(dve, tiles_all[:, k * half:(k + 1) * half], psum[2 + k][:, 0:half], [t_b])
        n_steps = small[:, 134:135]
        tile_hits = reg_a[:, 4000:4000 + STEPS_PAD]
        t = dve.do(lambda e: e.tensor_scalar(tile_hits, tiles_all, part, 0.0, ALU.is_le, ALU.add, accum_out=n_steps), [t])
        n_steps_i = small[:, 135:136].bitcast(I32)
        t = ts(n_steps_i, n_steps, -1.0, None, ALU.add, after=[t])
        t = dve.do(lambda e: e.tensor_scalar(n_steps_i, n_steps_i, GROUP.bit_length() - 1, None,
                                             ALU.arith_shift_right), [t])
        t = sp.dma(lambda e: e.dma_start(group_dram, n_steps_i[0:NODE_TILES, :]), store_done, [t])
        sp.dma(lambda e: e.dma_start(group_row[:, :], group_dram.rearrange("s k -> k s")), load2_done, [t])

        NI, NF = 4, 3
        ints = reg_x[:, 0:STEP_BLOCKS * NI * P].bitcast(I32).rearrange("p (b f) -> p b f", b=STEP_BLOCKS)
        flts = reg_x[:, STEP_BLOCKS * NI * P:STEP_BLOCKS * (NI + NF) * P].rearrange("p (b f) -> p b f", b=STEP_BLOCKS)
        conv = reg_acc[:, 0:STEP_BLOCKS * NI * P].rearrange("p (b f) -> p b f", b=STEP_BLOCKS)
        for b in range(STEP_BLOCKS):
            for out, table in ((ints[:, b, :], io["edge_ints"]), (flts[:, b, :], io["edge_floats"])):
                t_rows = pool.dma(lambda e, out=out, table=table, b=b: e.indirect_dma_start(
                    out, None, table, bass.IndirectOffsetOnAxis(ap=chunk_idx[:, b:b + 1], axis=0)),
                    table_done, [t_idx])
        masks = reg_b[:, 0:2 * STEPS_PAD].rearrange("p (k t) -> p k t", k=2)
        start_mask, end_mask = masks[:, 0, :], masks[:, 1, :]
        dst_before, dst_behind, flag, is_valid = (
            reg_x[:, k * STEPS_PAD:(k + 1) * STEPS_PAD] for k in range(8, 12))
        freed = {}
        for b in range(STEP_BLOCKS):
            w = min(P, STEPS_PAD - b * P)
            cols = slice(b * P, b * P + w)
            t_src = copy(dve, conv[:, b, 0:P], ints[:, b, 0:P], [t_rows])
            t_dst = ts(conv[:, b, P:4 * P], ints[:, b, P:4 * P], first_node[:, b:b + 1], None, ALU.subtract,
                       after=[t_first])
            at = flts[:, b, 0:2 * P].rearrange("p (j k) -> p k j", k=2)
            jobs = [(conv[:, b, 0:P], src_idx), (conv[:, b, P:2 * P], dst_loc),
                    (conv[:, b, 2 * P:3 * P], dst_before), (conv[:, b, 3 * P:4 * P], dst_behind),
                    (at[:, 0, :], attr0), (at[:, 1, :], attr1), (flts[:, b, 2 * P:3 * P], edge_w)]
            for n, (a, out) in enumerate(jobs):
                k = (b * len(jobs) + n) % 8
                t = transpose(psum[k][:, 0:P], a, [t_dst, t_rows] + ([freed[k]] if k in freed else []))
                freed[k] = t_tab = copy(dve, out[:, cols], psum[k][:, 0:w], [t])
        t = ts(flag, dst_loc[:, :], 0.0, None, ALU.is_ge, after=[t_tab])
        t = stt(is_valid, dst_loc[:, :], float(P), flag, ALU.is_lt, ALU.mult, [t])
        ts(cap, is_valid, -2.0 * LOW, LOW, ALU.mult, ALU.add, after=[t])
        for other, mask in ((dst_before, start_mask), (dst_behind, end_mask)):
            t = tt(flag, dst_loc[:, :], other, ALU.not_equal, [dve.last()])
            t = stt(mask, flag, LOW, is_valid, ALU.mult, ALU.mult, [t])
        counts = reg_x[:, 0:2 * STEPS_PAD]
        t = ts(counts, reg_b[:, 0:2 * STEPS_PAD], 0.0, None, ALU.is_lt, after=[t])
        run_masks = reg_b[0:1, 2 * STEPS_PAD:4 * STEPS_PAD].rearrange("p (k t) -> p k t", k=2)
        ones_col = reg_x[:, 2 * STEPS_PAD:2 * STEPS_PAD + 1]
        t = dve.do(lambda e: e.memset(ones_col, 1.0), [t])
        quarter = STEPS_PAD // 2
        for k in range(4):
            t_c = mm(psum[k][0:1, 0:quarter], ones_col, counts[:, k * quarter:(k + 1) * quarter], after=[t])
        for k in range(4):
            t = ts(reg_b[0:1, 2 * STEPS_PAD + k * quarter:2 * STEPS_PAD + (k + 1) * quarter],
                   psum[k][0:1, 0:quarter], 1.0, LOW, ALU.min, ALU.mult, after=[t_c])
        head_starts = reg_b[0:1, 4 * STEPS_PAD:4 * STEPS_PAD + GROUPS]
        t = copy(dve, head_starts, run_masks[:, 0, ::GROUP], [t])
        dve.do(lambda e: e.memset(run_masks[:, 0, ::GROUP], LOW), [t])
        dve.do(lambda e: e.memset(run_masks[:, 1, GROUP - 1::GROUP], LOW))
        goes_on = reg_x[0:1, 2000:2000 + GROUPS]
        going = reg_x[0:1, 2100:2100 + GROUPS]
        t = ts(goes_on, start_mask[0:1, ::GROUP], 0.0, None, ALU.is_equal, after=[dve.last()])
        t = tt(goes_on, goes_on, is_valid[0:1, ::GROUP], ALU.mult, [t])
        t = stt(going, dst_loc[0:1, ::GROUP], 1.0, goes_on, ALU.add, ALU.mult, [t])
        t = ts(going, going, -1.0, None, ALU.add, after=[t])
        t = mm(psum[4][:, 0:GROUPS], ones_row, going, after=[t])
        carried = reg_b[:, 4 * STEPS_PAD + 64:4 * STEPS_PAD + 64 + GROUPS]
        ts(carried, psum[4][:, 0:GROUPS], part, None, ALU.is_equal, after=[t])
        phase_end()

        x_rows = io["x"][0:FULL_TILES * P, :].rearrange("(t p) f -> p t f", p=P)

        def load_x(after=()):
            t = dve.do(lambda e: e.memset(x_sb[:, FULL_TILES, :], 0.0), after)
            load(x_sb[0:TAIL_ROWS, FULL_TILES, :], io["x"][FULL_TILES * P:NODES, :], [t])
            return load(x_sb[:, 0:FULL_TILES, :], x_rows, after)

        def score_weights(w_ext, w, att, where, after):
            prod = reg_a[:, 0:2 * FEAT].rearrange("p (k f) -> p k f", k=2)
            t = tt(prod, w, bcast(att, 1, [P, 2, FEAT]), ALU.mult, after)
            return dve.do(lambda e: e.tensor_reduce(
                w_ext[:, :, where:where + HEADS0], prod.rearrange("p k (h d) -> p k h d", h=HEADS0), AXX, ALU.add), [t])

        w0 = reg_w[:, 0:2 * ACC_W].rearrange("p (k f) -> p k f", k=2)
        att = reg_w[:, 2 * ACC_W:2 * ACC_W + 2 * FEAT]
        w_rows = io["w0"].rearrange("(k p) f -> p k f", p=P)
        load(w0[:, :, 0:FEAT], w_rows)
        for n, name in enumerate(("att_src", "att_dst")):
            load(att[:, n * FEAT:(n + 1) * FEAT], io[name].partition_broadcast(P))
        t = load_x()
        t = score_weights(w0, w0[:, :, 0:FEAT], att[:, 0:FEAT], FEAT, [t, tuple(load_done)])
        t_w0 = score_weights(w0, w0[:, :, 0:FEAT], att[:, FEAT:2 * FEAT], FEAT + HEADS0, [t])

        def matmul_stages(source, k_chunks, weights, width, turned, ready, banks=(0, 1, 2, 3)):
            t_turn, t_copy, t_mm, used = {}, {}, {}, {}
            two = turned.rearrange("p (s f) -> p s f", s=2)

            def turn(j):
                for k in range(k_chunks):
                    t_turn[j] = transpose(psum[banks[j % 2]][:, k * P:(k + 1) * P], source(j)[:, k * P:(k + 1) * P],
                                          ready(j) + ([t_copy[j - 2]] if j >= 2 else []))

            def keep(j):
                t_copy[j] = copy(act, two[:, j % 2, :], psum[banks[j % 2]][:, 0:k_chunks * P],
                                 [t_turn[j]] + ([t_mm[j - 2]] if j >= 2 else []))

            def multiply(j):
                for k in range(k_chunks):
                    t_mm[j] = mm(psum[banks[2 + j % 2]][:, 0:width], two[:, j % 2, k * P:(k + 1) * P], weights[:, k, :],
                                 k == 0, k == k_chunks - 1,
                                 [t_copy[j]] + ([used[j - 2]] if j >= 2 else []))

            return turn, keep, multiply, t_mm, used, banks

        turned = reg_a[:, 1024:1024 + 4 * P]
        turn, keep, multiply, t_mm, used, banks = matmul_stages(
            lambda j: x_sb[:, j, :], 2, w0, ACC_W, turned, lambda j: [t_w0, tuple(load_done)])

        def keep_h(j):
            copy(dve, acc[:, j, :], psum[banks[2 + j % 2]][:, 0:ACC_W], [t_mm[j]])
            used[j] = copy(dve, adst[:, j * HEADS0:(j + 1) * HEADS0],
                           psum[banks[2 + j % 2]][:, FEAT + HEADS0:ACC_W])

        pipeline(NODE_TILES, [turn, keep, multiply, keep_h])
        for a in range(0, NODE_TILES, 7):
            sp.dma(lambda e, a=a: e.dma_start(node_rows(tab_h0, a, a + 7), acc[:, a:a + 7, 0:ROW0]),
                   store_done, [dve.last()])
        dve.do(lambda e: e.memset(reg_acc[:, :], 0.0), [tuple(store_done)])
        phase_end()

        regs = {}

        def load_tiles(eng, t0, n):
            def make(e):
                if eng not in regs:
                    regs[eng] = [e.alloc_register(f"tile{k}") for k in range(16)]
                e.load(regs[eng][0:n], tile_row[0:1, t0:t0 + n])
            eng.plain(make)

        def tile_value(eng, e, t):
            return e.snap(regs[eng][t % 16], min_val=0, max_val=NODE_TILES - 1)

        def distances(out, t, after):
            return activate(out, iota_row[:, :], ACT.Abs, after, scale=-1.0, bias=dst_loc[:, t:t + 1])

        def one_hots(out, after):
            return activate(out, out, ACT.Relu, after, scale=-1.0, bias=1.0)

        def scan(out, mask, data, initial, after=()):
            return dve.do(lambda e: e.tensor_tensor_scan(out, mask, data, initial, ALU.add, ALU.max), after)

        def leaky(v, after):
            return stt(v, v, 0.2, v, ALU.mult, ALU.max, after)

        n_hot, n_bank, lag = 4, 6, 2
        rows = reg_a[:, 0:n_gather * FEAT].rearrange("p (s f) -> p s f", f=FEAT)
        hots = reg_a[:, n_gather * FEAT:n_gather * FEAT + n_hot * P].rearrange("p (s f) -> p s f", f=P)
        def add_product(i, bank, width, after):
            if i % 16 == 0:
                load_tiles(dve, i, 16)

            def make(e):
                a = reg_acc[:, bass.DynSlice(tile_value(dve, e, i) * ACC_W, width)]
                return e.tensor_tensor(a, a, bank[:, 0:width], ALU.add)
            return dve.do(make, after)

        def edge_pass(table, kind, extra=0, weights=None):
            width = FEAT + extra
            t_got, t_hot, t_rhs, t_mm, t_add, t_rev = {}, {}, {}, {}, {}, {}
            row_w = table.shape[1]

            def fetch(i):
                free = t_mm.get(i - n_gather)
                t_got[i] = gather(rows[:, i % n_gather, 0:row_w], table, i, gather_done[i % n_gather],
                                  [free] if free else [])

            def prepare(i):
                hot, row = hots[:, i % n_hot, :], rows[:, i % n_gather, :]
                free = [t_mm[i - n_hot]] if i >= n_hot else []
                if kind == "weighted":
                    t_hot[i] = ts(hot, iota_row[:, :], dst_loc[:, i:i + 1], edge_w[:, i:i + 1], ALU.is_equal,
                                  ALU.mult, after=free)
                else:
                    t_hot[i] = ts(hot, iota_row[:, :], dst_loc[:, i:i + 1], None, ALU.is_equal, after=free)
            def product(i):
                bank = psum[i % n_bank]
                hot = hots[:, i % n_hot, :]
                rhs = rows[:, i % n_gather, :]
                after = [t_hot[i], t_rhs.get(i, t_got[i])] + ([t_add[i - n_bank]] if i >= n_bank else [])
                t_mm[i] = mm(bank[:, 0:FEAT], hot, rhs, after=after)
                if extra:
                    t_mm[i] = mm(bank[:, FEAT:width], hot, weights[:, i, 0:extra])

            def add(i):
                t_add[i] = add_product(i, psum[i % n_bank], width, [t_mm[i]] + ([t_add[i - 1]] if i else []))

            for i in range(STEPS + lag):
                if i < STEPS:
                    fetch(i)
                    prepare(i)
                    product(i)
                if i >= lag:
                    add(i - lag)
            phase_end()

        group = 7
        groups = NODE_TILES // group
        scratch = reg_b[:, 0:group * FEAT].rearrange("p (t f) -> p t f", f=FEAT)
        stats = reg_b[:, 4096:4096 + NODE_TILES * 6].rearrange("p (t k) -> p t k", k=6)
        moments = reg_b[:, 4500:4500 + NODE_TILES * 2].rearrange("p (t k) -> p t k", k=2)
        rstd = reg_b[:, 4700:4700 + NODE_TILES]
        shift = reg_b[:, 4800:4800 + NODE_TILES]
        recip = reg_b[:, 5000:5000 + NODE_TILES * HEADS0].rearrange("p (t h) -> p t h", h=HEADS0)

        def eps_rsqrt(out, a, eps, after):
            t = ts(out, a, eps, None, ALU.add, after=after)
            t = activate(out, out, ACT.Sqrt, [t])
            return dve.do(lambda e: e.reciprocal(out, out), [t])

        def normalise(src, out, after=()):
            for j in range(NODE_TILES):
                t = dve.do(lambda e, j=j: e.bn_stats(stats[:, j, :], src(j)), after)
            for j in range(NODE_TILES):
                t = dve.do(lambda e, j=j: e.bn_aggr(moments[:, j, :], stats[:, j, :]), [t] if not j else [])
            t = eps_rsqrt(rstd, moments[:, :, 1], LN_EPS, [t])
            t = stt(shift, moments[:, :, 0], -1.0, rstd, ALU.mult, ALU.mult, [t])
            for j in range(NODE_TILES):
                t = activate(out(j), src(j), ACT.Identity, [t], scale=rstd[:, j:j + 1], bias=shift[:, j:j + 1])
            return t

        def load_vectors(names, at):
            out = []
            for name in names:
                n = io[name].shape[-1]
                load(reg_w[:, at:at + n], io[name].partition_broadcast(P))
                out.append(reg_w[:, at:at + n])
                at += n
            return out

        def heads_mean(n_heads, eps, out_dim):
            r = recip[:, :, 0:n_heads]
            t = ts(r, acc[:, :, FEAT:FEAT + n_heads], eps, None, ALU.add)
            t = dve.do(lambda e: e.reciprocal(r, r), [t])
            for j in range(NODE_TILES):
                v = acc[:, j, 0:FEAT].rearrange("p (h d) -> p h d", h=n_heads)
                t_last = tt(v, v, bcast(r[:, j, :], 2, [P, n_heads, out_dim]), ALU.mult, [t])
            return t_last

        def store_table(table, view, after):
            for a in range(0, NODE_TILES, group):
                sp.dma(lambda e, a=a: e.dma_start(node_rows(table, a, a + group), view[:, a:a + group, :]),
                       store_done, after)

        def heads_pass():
            S, H, D = GROUP, HEADS0, HEAD0_DIM
            width = FEAT + H + 1
            rows0 = reg_x[:, 0:3 * S * width].rearrange("p (s f) -> p s f", f=width)
            hots = reg_a[:, 0:2 * S * P].rearrange("p (s f) -> p s f", f=P)
            hots_t = reg_a[:, 2 * S * P:2 * S * P + 1024].rearrange("p (s f) -> p s f", s=2)
            at_b = [4 * STEPS_PAD + 128]

            def take(width, rows=P):
                at_b[0] += width
                return reg_b[0:rows, at_b[0] - width:at_b[0]]

            upright = take(3 * P)
            turned3 = take(3 * P)
            first = take(2 * P)
            second = take(2 * P)
            dst_part = take(P)
            both = take(2 * P)
            begin_col = take(2)
            node_both = take(2 * H)
            shrink = take(H)
            step_masks, tails, states, begins = (take(2 * P, rows=1) for _ in range(4))
            assert at_b[0] <= 7488
            level = small[0:1, 400:400 + 4 * H].rearrange("p (k f) -> p k f", k=2)
            t_i0 = dve.do(lambda e: e.memset(level[:, 0, :], LOW))
            t_i1 = dve.do(lambda e: e.memset(begins, LOW))
            t_i2 = dve.do(lambda e: e.memset(rows0[:, :, ROW0:width], 1.0))
            n_bank = 3
            bank_t, bank_d, bank_3, bank_c = (psum[3], psum[4]), psum[5], psum[6], psum[7]
            t_got, t_rhs, t_mm, t_add, t_weight, t_shrink, t_hot, t_scaled = {}, {}, {}, {}, {}, {}, {}, {}
            t_turned, t_kept, t_exp, t_level = {}, {}, {}, {}
            t_level[0] = t_i0

            def fetch(g):
                for t in range(g * S, (g + 1) * S):
                    free = [t_mm[t - 3 * S]] if g >= 3 else []
                    t_got[g] = gather(rows0[:, t % (3 * S), 0:ROW0], tab_h0, t, group_done[g % 3], free)

            def chain(g):
                block = rows0[:, g % 3 * S:(g % 3 + 1) * S, :]
                cols = slice(g * S, (g + 1) * S)
                tok = {}
                sh = "p (s h) -> p s h"

                def distance(k):
                    for t in (g * S + k, g * S + k + 1):
                        tok["a"] = distances(hots[:, t % (2 * S), :], t, [t_mm[t - 2 * S]] if g >= 2 else [])

                def hot(c):
                    a = (g * S + 4 * c) % (2 * S)
                    t_hot[g, c] = one_hots(hots[:, a:a + 4, :], [tok["a"]])

                def hot_turn(c):
                    for k in range(4):
                        t_turned[c] = transpose(bank_t[c % 2][:, k * P:(k + 1) * P],
                                                hots[:, (g * S + 4 * c + k) % (2 * S), :],
                                                [t_hot[g, c]] + ([t_kept[c % 2]] if c % 2 in t_kept else []))

                def hot_keep(c):
                    t_kept[c % 2] = copy(act, hots_t[:, c % 2, :], bank_t[c % 2][:, :],
                                         [t_turned[c]] + ([t_exp[c % 2]] if c % 2 in t_exp else []))

                def dst_mm(c):
                    if c == 0:
                        load_tiles(pe, g * S, S)
                    for k in range(4):
                        t = g * S + 4 * c + k
                        t_exp[c % 2] = pe.do(lambda e, t=t, c=c, k=k: e.matmul(
                            bank_d[:, t % S * H:(t % S + 1) * H], hots_t[:, c % 2, k * P:(k + 1) * P],
                            adst[:, bass.DynSlice(tile_value(pe, e, t) * H, H)], start=True, stop=True),
                            [t_kept[c % 2]] + ([t_part[0]] if t_part else []))

                def upright_masks():
                    tok["k"] = copy(act, step_masks.rearrange("p (k h s) -> p k h s", k=2, h=H),
                                    bcast(run_masks[:, :, cols], 2, [1, 2, H, S]), [t_level[g]])
                    tok["m"] = copy(act, upright[:, 0:2 * P].rearrange("p (k s h) -> p k s h", k=2, h=H),
                                    bcast(masks[:, :, cols], 3, [P, 2, S, H]), [t_u[0]] if t_u else [])
                    tok["s"] = tt(upright[:, 2 * P:3 * P].rearrange(sh, h=H), block[:, :, FEAT:ROW0],
                                  bcast(cap[:, cols], 2, [P, S, H]), ALU.min, [t_got[g]])

                def turn3():
                    for k in range(3):
                        tok["3"] = transpose(bank_3[:, k * P:(k + 1) * P], upright[:, k * P:(k + 1) * P],
                                             [tok["m"], tok["s"]])

                def keep3():
                    tok["3"] = copy(act, turned3, bank_3[:, 0:3 * P], [tok["3"], dve.last()])

                def first_round():
                    scan(first[:, 0:P], turned3[:, 0:P], turned3[:, 2 * P:3 * P], LOW, [tok["3"]])
                    tok["f"] = scan(first[:, P:2 * P][:, ::-1], turned3[:, P:2 * P][:, ::-1],
                                    turned3[:, 2 * P:3 * P][:, ::-1], LOW)

                def turn_tails():
                    for k in range(2):
                        tok["r"] = transpose(bank_c[0:1, k * P:(k + 1) * P], first[:, P - 1 + k:P + k], [tok["f"]])

                def keep_tails():
                    tok["r"] = copy(act, tails.rearrange("p (k h s) -> p k h s", k=2, h=H),
                                    bank_c[0:1, 0:2 * P].rearrange("p (k s h) -> p k h s", k=2, h=H), [tok["r"]])

                def over_steps():
                    ft = tails[:, 0:P].rearrange("p (h s) -> p h s", h=H)[:, :, 0]
                    t = stt(ft, level[:, g % 2, 0:H], head_starts[:, g:g + 1], ft, ALU.add, ALU.max,
                            [tok["r"], t_level[g]])
                    scan(states[:, P:2 * P][:, ::-1], step_masks[:, P:2 * P][:, ::-1], tails[:, P:2 * P][:, ::-1], LOW,
                         [tok["k"]])
                    tok["o"] = scan(states[:, 0:P], step_masks[:, 0:P], tails[:, 0:P], LOW, [t])

                def hand_on():
                    st = states.rearrange("p (k h s) -> p k s h", k=2, h=H)
                    be = begins.rearrange("p (k s h) -> p k s h", k=2, h=H)
                    copy(act, be[:, 0, 1:S, :], st[:, 0, 0:S - 1, :], [tok["o"]])
                    copy(act, be[:, 1, 0:S - 1, :], st[:, 1, 1:S, :])
                    tok["b"] = copy(act, be[:, 0, 0, :], level[:, g % 2, 0:H])
                    tok["l"] = tt(level[:, g % 2, H:2 * H], level[:, g % 2, 0:H], st[:, 1, 0, :], ALU.max, [tok["o"]])
                    t_level[g + 1] = copy(dve, level[:, (g + 1) % 2, 0:H], st[:, 0, S - 1, :])

                def turn_begins():
                    for k in range(2):
                        transpose(bank_c[:, 256 + k:257 + k], begins[:, k * P:(k + 1) * P], [tok["b"], t_i1])
                    tok["c"] = mm(bank_c[:, 264:264 + 2 * H], ones_row, level[:, g % 2, :], after=[tok["l"]])

                def keep_begins():
                    tok["c"] = copy(act, begin_col, bank_c[:, 256:258], [tok["c"]])

                def keep_part():
                    tok["d"] = t_part_new = copy(act, dst_part, bank_d[:, 0:S * H], [t_exp[1]])
                    t_part[:] = [t_part_new]

                def node_levels():
                    def make(e):
                        if "head" not in regs:
                            regs["head"] = e.alloc_register("head_tile")
                        e.load(regs["head"], tile_row[0:1, g * S:g * S + 1])
                        v = e.snap(regs["head"], min_val=0, max_val=NODE_TILES - 1)
                        return e.tensor_tensor(node_both.rearrange("p (k h) -> p k h", k=2),
                                               bank_c[:, 264:264 + 2 * H].rearrange("p (k h) -> p k h", k=2),
                                               bcast(adst[:, bass.DynSlice(v * H, H)], 1, [P, 2, H]), ALU.add)
                    tok["n"] = dve.do(make, [tok["c"]])

                def second_round():
                    scan(second[:, 0:P], turned3[:, 0:P], turned3[:, 2 * P:3 * P], begin_col[:, 0:1], [tok["c"]])
                    tok["x"] = scan(second[:, P:2 * P][:, ::-1], turned3[:, P:2 * P][:, ::-1],
                                    turned3[:, 2 * P:3 * P][:, ::-1], begin_col[:, 1:2])

                def larger():
                    tok["n"] = leaky(node_both, [tok["n"]])
                    tok["x"] = tt(second[:, 0:P], second[:, 0:P], second[:, P:2 * P], ALU.max, [tok["x"]])
                    tok["n"] = tt(shrink, node_both[:, 0:H], node_both[:, H:2 * H], ALU.subtract, [tok["n"]])
                    tok["e"] = activate(shrink, shrink, ACT.Exp, [tok["n"]])

                def turn_larger():
                    tok["x"] = transpose(bank_c[:, 3 * P:4 * P], second[:, 0:P], [tok["x"]])
                    tok["u"] = tt(both[:, 0:P], upright[:, 2 * P:3 * P], dst_part, ALU.add, [tok["d"]])
                    t_u[:] = [tok["u"]]

                def add_dst():
                    tok["u"] = tt(both[:, P:2 * P], bank_c[:, 3 * P:4 * P], dst_part, ALU.add, [tok["x"]])
                    tok["n"] = ts(shrink, shrink, -1.0, carried[:, g:g + 1], ALU.add, ALU.mult, after=[tok["e"]])

                def bend():
                    tok["u"] = leaky(both, [tok["u"]])
                    t_shrink[g] = ts(shrink, shrink, 1.0, None, ALU.add, after=[tok["n"]])

                def below():
                    tok["u"] = tt(both[:, 0:P], both[:, 0:P], both[:, P:2 * P], ALU.subtract, [tok["u"]])

                def exps():
                    t_weight[g] = activate(block[:, :, FEAT:ROW0], both[:, 0:P].rearrange(sh, h=H), ACT.Exp,
                                           [tok["u"], t_i2])

                def c(make, *args):
                    return lambda: make(*args)

                return [
                    ([upright_masks, c(distance, 0)], []),
                    ([turn3, keep3, c(distance, 2), c(hot, 0)], []),
                    ([first_round, c(distance, 4)], [c(hot_turn, 0), c(hot_keep, 0)]),
                    ([turn_tails, keep_tails, c(distance, 6), c(hot, 1)], [c(dst_mm, 0)]),
                    ([c(distance, 8)], [c(hot_turn, 1), c(hot_keep, 1)]),
                    ([over_steps, c(distance, 10), c(hot, 2)], [c(dst_mm, 1)]),
                    ([hand_on], [c(hot_turn, 2), c(hot_keep, 2)]),
                    ([turn_begins, keep_begins, c(distance, 12)], [c(dst_mm, 2)]),
                    ([c(distance, 14), c(hot, 3)], [c(hot_turn, 3)]),
                    ([second_round, node_levels, c(hot_keep, 3)], [c(dst_mm, 3)]),
                    ([larger, keep_part], []),
                    ([turn_larger], []),
                    ([add_dst], []),
                    ([bend], []),
                    ([below, exps], []),
                ]

            t_part, t_u = [], []

            def rescale(g):
                i = g * S
                load_tiles(dve, i, 16)

                def at(e, a, b):
                    return reg_acc[:, bass.DynSlice(tile_value(dve, e, i) * ACC_W + a, b - a)]

                def sums(e):
                    v = at(e, 0, FEAT).rearrange("p (h d) -> p h d", h=H)
                    return e.tensor_tensor(v, v, bcast(shrink, 2, [P, H, D]), ALU.mult)

                def denominators(e):
                    v = at(e, FEAT, FEAT + H)
                    return e.tensor_tensor(v, v, shrink, ALU.mult)
                dve.do(sums, [t_shrink[g], t_add[i - 1]])
                t_scaled[g] = dve.do(denominators)

            def prepare(i):
                g = i // S
                v = rows0[:, i % (3 * S), 0:FEAT].rearrange("p (h d) -> p h d", h=H)
                t_rhs[i] = tt(v, v, bcast(rows0[:, i % (3 * S), FEAT:ROW0], 2, [P, H, D]), ALU.mult, [t_weight[g]])

            def product(i):
                bank, hot = psum[i % n_bank], hots[:, i % (2 * S), :]
                t_mm[i] = mm(bank[:, 0:width], hot, rows0[:, i % (3 * S), :],
                             after=[t_rhs[i]] + ([t_add[i - n_bank]] if i >= n_bank else []))

            def add(i):
                g = i // S
                fresh = g and i % S == 0
                if fresh:
                    rescale(g)
                before = [t_scaled[g]] if fresh else [t_add[i - 1]] if i else []
                t_add[i] = add_product(i, psum[i % n_bank], width, [t_mm[i]] + before)

            fetch(0)
            fetch(1)
            for ahead, behind in chain(0):
                for link in ahead + behind:
                    link()
            for g in range(GROUPS):
                if g + 2 < GROUPS:
                    fetch(g + 2)
                steps = chain(g + 1) if g + 1 < GROUPS else []
                for k in range(S):
                    i = g * S + k
                    ahead, behind = steps[k] if k < len(steps) else ([], [])
                    prepare(i)
                    for link in ahead:
                        link()
                    product(i)
                    for link in behind:
                        link()
                    if i >= lag:
                        add(i - lag)
            for i in range(STEPS_PAD - lag, STEPS_PAD):
                add(i)
            phase_end()

        heads_pass()
        load_x()
        (bias0,) = load_vectors(["bias0"], 0)
        t = copy(dve, dinv[:, :], acc[:, :, FEAT + HEADS0])
        eps_rsqrt(dinv[:, :], dinv[:, :], 1.0, [t])
        t = heads_mean(HEADS0, 1e-16, HEAD0_DIM)
        for a in range(0, NODE_TILES, group):
            v, x = acc[:, a:a + group, 0:FEAT], x_sb[:, a:a + group, :]
            t = tt(v, v, bcast(bias0, 1, [P, group, FEAT]), ALU.add, [t, tuple(load_done)])
            t = stt(x, v, 0.0, x, ALU.max, ALU.add, [t])
        t = normalise(lambda j: x_sb[:, j, :], lambda j: x_sb[:, j, :], [t])
        for j in range(NODE_TILES):
            t = act.do(lambda e, j=j: e.mul(acc[:, j, 0:FEAT], x_sb[:, j, :], dinv[:, j:j + 1]), [t])
        store_table(tab_x1, acc[:, :, 0:FEAT], [t])
        phase_end()

        edge_pass(tab_x1, "plain")
        w1 = reg_w[:, 0:2 * HIDDEN].rearrange("p (k f) -> p k f", k=2)
        w2 = reg_w[:, 2 * HIDDEN:4 * HIDDEN].rearrange("p (k f) -> p k f", k=4)
        load(w1, io["w1"].rearrange("(k p) f -> p k f", p=P))
        load(w2, io["w2"].rearrange("(k p) f -> p k f", p=P))
        bias1, gamma1, beta1 = load_vectors(["b1", "gamma1", "beta1"], 4 * HIDDEN)
        t_loads = tuple(load_done)
        turned = reg_a[:, 0:4 * P]
        turn, keep, multiply, t_mm, used, banks = matmul_stages(
            lambda j: acc[:, j, 0:FEAT], 2, w1, HIDDEN, turned, lambda j: [t_loads])
        hid = reg_a[:, 1024:1024 + 4 * HIDDEN].rearrange("p (s f) -> p s f", s=4)
        t_stat, t_norm, t_hid = {}, {}, {}

        def hidden_in(j):
            h = hid[:, j % 4, :]
            used[j] = t = stt(h, psum[banks[2 + j % 2]][:, :], dinv[:, j:j + 1], bias1, ALU.mult, ALU.add,
                              [t_mm[j], t_loads] + ([t_turn2[j - 4]] if j >= 4 else []))
            t = dve.do(lambda e: e.bn_stats(stats[:, j, :], h), [t])
            t = dve.do(lambda e: e.bn_aggr(moments[:, j, :], stats[:, j, :]), [t])
            t = ts(rstd[:, j:j + 1], moments[:, j, 1:2], LN_EPS, None, ALU.add, after=[t])
            t_stat[j] = activate(rstd[:, j:j + 1], rstd[:, j:j + 1], ACT.Sqrt, [t])

        def hidden_norm(j):
            h = hid[:, j % 4, :]
            t = dve.do(lambda e: e.reciprocal(rstd[:, j:j + 1], rstd[:, j:j + 1]), [t_stat[j]])
            t = ts(h, h, moments[:, j, 0:1], rstd[:, j:j + 1], ALU.subtract, ALU.mult, after=[t])
            t = tt(h, h, gamma1, ALU.mult, [t])
            t_norm[j] = tt(h, h, beta1, ALU.add, [t])
            t_hid[j] = activate(h, h, ACT.Relu, [t_norm[j]])

        turned2 = reg_a[:, 3072:3072 + 8 * P]
        turn2, keep2, multiply2, t_mm2, used2, banks2 = matmul_stages(
            lambda j: hid[:, j % 4, :], 4, w2, FEAT, turned2, lambda j: [t_hid[j]], banks=(4, 5, 6, 7))
        t_turn2 = {}

        def turn2_noted(j):
            turn2(j)
            t_turn2[j] = pe.last()

        def hidden_out(j):
            used2[j] = act.do(lambda e: e.mul(acc[:, j, 0:FEAT], psum[banks2[2 + j % 2]][:, 0:FEAT], dinv[:, j:j + 1]),
                              [t_mm2[j]])

        pipeline(NODE_TILES, [turn, keep, multiply, hidden_in, hidden_norm, turn2_noted, keep2, multiply2, hidden_out])
        store_table(tab_h2, acc[:, :, 0:FEAT], [act.last()])
        phase_end()

        edge_pass(tab_h2, "plain")
        bias2, gamma2, beta2 = load_vectors(["b2", "gamma2", "beta2"], 0)
        t = dve.last()
        for j in range(NODE_TILES):
            v = acc[:, j, 0:FEAT]
            t = stt(v, v, dinv[:, j:j + 1], bias2, ALU.mult, ALU.add, [tuple(load_done)])
        t = normalise(lambda j: acc[:, j, 0:FEAT], lambda j: acc[:, j, 0:FEAT], [t])
        for a in range(0, NODE_TILES, group):
            v, x = acc[:, a:a + group, 0:FEAT], x_sb[:, a:a + group, :]
            t = tt(v, v, bcast(gamma2, 1, [P, group, FEAT]), ALU.mult, [t])
            t = tt(v, v, bcast(beta2, 1, [P, group, FEAT]), ALU.add, [t])
            t = stt(x, v, 0.0, x, ALU.max, ALU.add, [t])
        t = normalise(lambda j: x_sb[:, j, :], lambda j: x_sb[:, j, :], [t])
        store_table(tab_x2, x_sb, [t])
        dve.do(lambda e: e.memset(reg_acc[:, :], 0.0))
        phase_end()

        edge_pass(tab_x2, "weighted")
        wl2 = reg_w[:, 0:2 * FEAT].rearrange("p (k f) -> p k f", k=2)
        load(wl2, io["w_l2"].rearrange("(k p) f -> p k f", p=P))
        (bias_l2,) = load_vectors(["b_l2"], 2 * FEAT)
        t_loads = tuple(load_done)
        turn, keep, multiply, t_mm, used, banks = matmul_stages(
            lambda j: acc[:, j, 0:FEAT], 2, wl2, FEAT, turned, lambda j: [t_loads])
        t_bias = {}

        def l2_out(j):
            v = acc[:, j, 0:FEAT]
            used[j] = t = tt(v, psum[banks[2 + j % 2]][:, 0:FEAT], bias_l2, ALU.add, [t_mm[j], t_loads])
            stt(x_sb[:, j, :], v, 0.0, x_sb[:, j, :], ALU.max, ALU.add, [t])

        pipeline(NODE_TILES, [turn, keep, multiply, l2_out])
        normalise(lambda j: x_sb[:, j, :], lambda j: x_sb[:, j, :], [dve.last()])
        phase_end()

        w3_w = ROW3
        w3 = reg_w[:, 0:2 * w3_w].rearrange("p (k f) -> p k f", k=2)
        raw = reg_w[0:OUT3, 512:512 + 2 * FEAT].rearrange("p (d f) -> p d f", d=2)
        attn_row = reg_w[0:HEADS3, 1024:1024 + OUT3]
        turner = reg_w[0:OUT3, 1100:1100 + OUT3 + HEADS3]
        load(raw[:, 0, :], io["w_fwd"])
        load(raw[:, 1, :], io["w_rev"])
        t = load(attn_row, io["attn"])
        t = transpose(psum[0][0:OUT3, 0:HEADS3], attn_row, [t])
        copy(dve, turner[:, OUT3:OUT3 + HEADS3], psum[0][0:OUT3, 0:HEADS3], [t])
        t = copy(dve, turner[:, 0:OUT3], ident[0:OUT3, 0:OUT3])
        for d in range(2):
            for k in range(2):
                bank = psum[1 + 2 * d + k]
                t_w = mm(bank[:, 0:OUT3 + HEADS3], raw[:, d, k * P:(k + 1) * P], turner, after=[t])
                copy(dve, w3[:, k, d * OUT3:(d + 1) * OUT3], bank[:, 0:OUT3], [t_w])
                copy(dve, w3[:, k, 2 * OUT3 + d * HEADS3:2 * OUT3 + (d + 1) * HEADS3], bank[:, OUT3:OUT3 + HEADS3])
        t_w3 = dve.last()
        for e in (pe, act):
            e.wait(t_w3)
        turn, keep, multiply, t_mm, used, banks = matmul_stages(
            lambda j: x_sb[:, j, :], 2, w3, w3_w, turned, lambda j: [])

        def l3_keep(j):
            used[j] = copy(dve, acc[:, j, 0:w3_w], psum[banks[2 + j % 2]][:, 0:w3_w], [t_mm[j]])

        pipeline(NODE_TILES, [turn, keep, multiply, l3_keep])
        store_table(tab_h3, acc[:, :, 0:ROW3], [dve.last()])
        dve.do(lambda e: e.memset(reg_acc[:, :], 0.0), [tuple(store_done)])
        phase_end()

        def mix_pass():
            rows3 = reg_a[:, 0:3 * GROUP * ROW3].rearrange("p (s f) -> p s f", f=ROW3)
            rings = reg_b[:, :]
            hots = rings[:, 3100:3100 + 12 * P].rearrange("p (s f) -> p s f", s=12)
            reverse = rings[:, 512:512 + 4 * OUT3].rearrange("p (s f) -> p s f", s=4)
            message = rings[:, 768:768 + 4 * OUT3].rearrange("p (s f) -> p s f", s=4)
            scaled = rings[:, 4700:4700 + 4 * (FEAT + HEADS3)].rearrange("p (s f) -> p s f", s=4)
            ghw = [P, GROUP, HEADS3]
            weight = rings[:, 2048:2048 + 3 * GROUP * HEADS3].rearrange("p (g t h) -> p g t h", g=3, h=HEADS3)
            part_score = rings[:, 2304:2304 + 2 * GROUP * HEADS3].rearrange("p (k t h) -> p k t h", k=2, h=HEADS3)
            top = rings[:, 2500:2500 + HEADS3]
            shrink = rings[:, 2510:2510 + HEADS3]
            run_top = rings[0:HEADS3, 2520:2520 + GROUPS + 1]
            diag = rings[0:HEADS3, 2580:2580 + HEADS3]
            ones4 = rings[0:HEADS3, 2600:2600 + P]
            tops = rings[:, 2800:2800 + GROUPS * HEADS3].rearrange("p (g h) -> p g h", h=HEADS3)
            bank_c = psum[7]
            dve.do(lambda e: e.memset(ones4, 1.0))
            t_init = dve.do(lambda e: e.memset(run_top[:, 0:1], LOW))
            width = FEAT + HEADS3
            t_got, t_rhs, t_mm, t_add, t_weight, t_shrink, t_rev, t_hot = {}, {}, {}, {}, {}, {}, {}, {}
            t_scaled, t_wcopy = {}, {}

            def fetch(g):
                for t in range(g * GROUP, (g + 1) * GROUP):
                    free = [t_rhs[t - 3 * GROUP]] if g >= 3 else []
                    t_got[g] = gather(rows3[:, t % (3 * GROUP), :], tab_h3, t, group_done[g % 3], free)

            def chain(g):
                block = rows3[:, g % 3 * GROUP:(g % 3 + 1) * GROUP, 2 * OUT3:]
                cols = slice(g * GROUP, (g + 1) * GROUP)
                w = weight[:, g % 3]
                tok = {}

                def scores():
                    tt(part_score[:, 0], block[:, :, 0:HEADS3], bcast(attr0[:, cols], 2, ghw), ALU.mult, [t_got[g]])
                    tok["s"] = tt(part_score[:, 1], block[:, :, HEADS3:], bcast(attr1[:, cols], 2, ghw), ALU.mult)

                def total():
                    tok["s"] = tt(w, part_score[:, 0], part_score[:, 1], ALU.add, [tok["s"]])

                def bend():
                    tok["s"] = leaky(w.rearrange("p t h -> p (t h)"), [tok["s"]])

                def slot_top():
                    tok["t"] = dve.do(lambda e: e.tensor_reduce(top, w.rearrange("p t h -> p h t"), AXX, ALU.max),
                                      [tok["s"]])

                def turn_top():
                    tok["t"] = transpose(bank_c[0:HEADS3, 0:P], top, [tok["t"]])

                def all_top():
                    tok["t"] = dve.do(lambda e: e.tensor_reduce(run_top[:, g + 1:g + 2], bank_c[0:HEADS3, 0:P], AXX,
                                                                ALU.max), [tok["t"], t_init])

                def so_far():
                    tok["t"] = tt(run_top[:, g + 1:g + 2], run_top[:, g:g + 1], run_top[:, g + 1:g + 2], ALU.max,
                                  [tok["t"]])

                def on_diagonal():
                    tok["t"] = ts(diag, ident[0:HEADS3, 0:HEADS3], run_top[:, g + 1:g + 2], None, ALU.mult,
                                  after=[tok["t"]])

                def to_all():
                    tok["t"] = mm(bank_c[:, 256:256 + HEADS3], ones4, diag, after=[tok["t"]])

                def keep_top():
                    tok["t"] = copy(dve, tops[:, g, :], bank_c[:, 256:256 + HEADS3], [tok["t"]])

                def below():
                    t = tt(w, w, bcast(tops[:, g, :], 1, ghw), ALU.subtract, [tok["t"]])
                    if g:
                        t = tt(shrink, tops[:, g - 1, :], tops[:, g, :], ALU.subtract)
                    tok["t"] = t

                def exps():
                    wf = w.rearrange("p t h -> p (t h)")
                    t_weight[g] = activate(wf, wf, ACT.Exp, [tok["t"]])
                    if g:
                        t_shrink[g] = activate(shrink, shrink, ACT.Exp, [tok["t"]])

                return [[scores], [total], [bend], [slot_top], [turn_top], [], [all_top], [so_far], [on_diagonal],
                        [to_all], [], [keep_top], [below], [exps]]

            def rescale(g):
                i = g * GROUP
                load_tiles(dve, i, 16)

                def at(e, a, b):
                    return reg_acc[:, bass.DynSlice(tile_value(dve, e, i) * ACC_W + a, b - a)]

                def sums(e):
                    v = at(e, 0, FEAT).rearrange("p (h d) -> p h d", h=HEADS3)
                    return e.tensor_tensor(v, v, bcast(shrink, 2, [P, HEADS3, OUT3]), ALU.mult)

                def denominators(e):
                    v = at(e, FEAT, width)
                    return e.tensor_tensor(v, v, shrink, ALU.mult)
                dve.do(sums, [t_shrink[g], t_add[i - 1]])
                t_scaled[g] = dve.do(denominators)

            def hot(i):
                t = distances(hots[:, i % 12, :], i, [t_mm[i - 12]] if i >= 12 else [])
                if i % 4 == 3:
                    t_hot[i // 4] = one_hots(hots[:, (i - 3) % 12:(i - 3) % 12 + 4, :], [t])

            def prepare(i):
                s, g = i % 4, i // GROUP
                row = rows3[:, i % (3 * GROUP), :]
                free = [t_mm[i - 4]] if i >= 4 else []
                t_rev[i] = act.do(lambda e: e.mul(reverse[:, s, :], row[:, OUT3:2 * OUT3], attr1[:, i:i + 1]),
                                  [t_got[g]] + free)
                t_msg = stt(message[:, s, :], row[:, 0:OUT3], attr0[:, i:i + 1], reverse[:, s, :], ALU.mult,
                            ALU.add, [t_rev[i]])
                t_wcopy[i] = copy(act, scaled[:, s, FEAT:width], weight[:, g % 3, i % GROUP, :], free)
                t_rhs[i] = tt(scaled[:, s, 0:FEAT].rearrange("p (h d) -> p h d", h=HEADS3),
                              bcast(message[:, s, :], 1, [P, HEADS3, OUT3]),
                              bcast(weight[:, g % 3, i % GROUP, :], 2, [P, HEADS3, OUT3]), ALU.mult,
                              [t_msg, t_weight[g]])

            def product(i):
                t_mm[i] = mm(psum[i % n_bank][:, 0:width], hots[:, i % 12, :], scaled[:, i % 4, :],
                             after=[t_hot[i // 4], t_rhs[i], t_wcopy[i]] +
                             ([t_add[i - n_bank]] if i >= n_bank else []))

            def add(i):
                g = i // GROUP
                if g and i % GROUP == 0:
                    rescale(g)
                t_add[i] = add_product(i, psum[i % n_bank], width,
                                       [t_mm[i], t_scaled[g] if i % GROUP == 0 and g else dve.last()]
                                       if i % GROUP == 0 else [t_mm[i], t_add[i - 1]])

            fetch(0)
            fetch(1)
            for links in chain(0):
                for link in links:
                    link()
            for i in range(8):
                hot(i)
            for g in range(GROUPS):
                if g + 2 < GROUPS:
                    fetch(g + 2)
                steps = chain(g + 1) if g + 1 < GROUPS else []
                for k in range(GROUP):
                    i = g * GROUP + k
                    prepare(i)
                    if k < len(steps):
                        for link in steps[k]:
                            link()
                    if i + 8 < STEPS_PAD:
                        hot(i + 8)
                    product(i)
                    if i >= lag:
                        add(i - lag)
            for i in range(STEPS_PAD - lag, STEPS_PAD):
                add(i)
            phase_end()
            return tops

        tops = mix_pass()
        factor = reg_a[:, 0:NODE_TILES * HEADS3].rearrange("p (t h) -> p t h", h=HEADS3)
        factor_r = reg_a[:, 256:256 + NODE_TILES * HEADS3].rearrange("p (t h) -> p t h", h=HEADS3)
        tops_flat = tops.rearrange("p g h -> p (g h)")
        group_regs = []

        def pick(d):
            def make(e):
                if not group_regs:
                    group_regs.extend(e.alloc_register(f"group{k}") for k in range(8))
                if d % 8 == 0:
                    n = min(8, NODE_TILES - d)
                    e.load(group_regs[0:n], group_row[0:1, d:d + n])
                v = e.snap(group_regs[d % 8], min_val=0, max_val=GROUPS - 1)
                return e.tensor_copy(factor[:, d, :], tops_flat[:, bass.DynSlice(v * HEADS3, HEADS3)])
            return dve.do(make)

        for d in range(NODE_TILES):
            t = pick(d)
        t = tt(factor, factor, bcast(tops[:, GROUPS - 1, :], 1, [P, NODE_TILES, HEADS3]), ALU.subtract, [t])
        t = activate(factor, factor, ACT.Exp, [t])
        den = acc[:, :, FEAT:FEAT + HEADS3]
        t = tt(den, den, factor, ALU.mult, [t])
        t = ts(den, den, 1e-10, None, ALU.add, after=[t])
        t = dve.do(lambda e: e.reciprocal(factor_r, den), [t])
        t = tt(factor, factor, factor_r, ALU.mult, [t])
        for j in range(NODE_TILES):
            v = acc[:, j, 0:FEAT].rearrange("p (h d) -> p h d", h=HEADS3)
            t_last = tt(v, v, bcast(factor[:, j, :], 2, [P, HEADS3, OUT3]), ALU.mult, [t])
        t = t_last
        for a in range(0, NODE_TILES, group):
            v, x = acc[:, a:a + group, 0:FEAT], x_sb[:, a:a + group, :]
            t = tt(x, v, x, ALU.add, [t])
        t = normalise(lambda j: x_sb[:, j, :], lambda j: x_sb[:, j, :], [t])
        out_rows = io["out"][0:FULL_TILES * P, :].rearrange("(t p) f -> p t f", p=P)
        out_done = [sem("s_out"), 0]
        sp.dma(lambda e: e.dma_start(out_rows, x_sb[:, 0:FULL_TILES, :]), out_done, [t])
        sp.dma(lambda e: e.dma_start(io["out"][FULL_TILES * P:NODES, :], x_sb[0:TAIL_ROWS, FULL_TILES, :]),
               out_done, [t])
        sp.wait(tuple(out_done), tuple(store_done))

        block = ctx.enter_context(nc.Block())

        @block.tensor
        def _(e):
            pe.replay(e)

        @block.vector
        def _(e):
            dve.replay(e)

        @block.scalar
        def _(e):
            act.replay(e)

        @block.gpsimd
        def _(e):
            pool.replay(e)

        @block.sync
        def _(e):
            sp.replay(e)


def kernel(x, src, dst, edge_attr_2, edge_weight, L0_gnn_W, L0_gnn_att_src, L0_gnn_att_dst, L0_gnn_bias, L1_gnn_W1,
           L1_gnn_b1, L1_gnn_gamma1, L1_gnn_beta1, L1_gnn_W2, L1_gnn_b2, L1_gnn_gamma2, L1_gnn_beta2, L2_gnn_W,
           L2_gnn_b, L3_gnn_W_forward, L3_gnn_W_reverse, L3_gnn_attn_forward):
    import concourse.bacc as bacc
    from concourse.bass_utils import run_bass_kernel_spmd

    fill = EDGES_PAD - EDGES
    src, dst = np.asarray(src), np.asarray(dst)
    attr, weight = np.asarray(edge_attr_2), np.asarray(edge_weight)
    none = np.full(1, -1, dst.dtype)
    dst_pad = np.concatenate([dst, np.full(fill, JUNK_NODE, dst.dtype)])
    edge_ints = np.concatenate([v.reshape(CHUNKS, P) for v in (
        np.concatenate([src, src[-fill:]]), dst_pad, np.concatenate([none, dst_pad[:-1]]),
        np.concatenate([dst_pad[1:], none]))], axis=1)
    edge_floats = np.concatenate([np.concatenate([attr, attr[-fill:]]).reshape(CHUNKS, 2 * P),
                                  np.concatenate([weight, weight[-fill:]]).reshape(CHUNKS, P)], axis=1)
    ins = {
        "x": x, "edge_ints": edge_ints, "edge_floats": edge_floats,
        "w0": np.asarray(L0_gnn_W).reshape(FEAT, FEAT), "att_src": np.asarray(L0_gnn_att_src).reshape(FEAT),
        "att_dst": np.asarray(L0_gnn_att_dst).reshape(FEAT), "bias0": L0_gnn_bias,
        "w1": L1_gnn_W1, "b1": L1_gnn_b1, "gamma1": L1_gnn_gamma1, "beta1": L1_gnn_beta1,
        "w2": L1_gnn_W2, "b2": L1_gnn_b2, "gamma2": L1_gnn_gamma2, "beta2": L1_gnn_beta2,
        "w_l2": L2_gnn_W, "b_l2": L2_gnn_b, "w_fwd": L3_gnn_W_forward, "w_rev": L3_gnn_W_reverse,
        "attn": np.asarray(L3_gnn_attn_forward).reshape(HEADS3, OUT3),
    }
    nc = bacc.Bacc("TRN2", target_bir_lowering=False, num_devices=1)
    arrays, io = {}, {}
    for name, a in ins.items():
        a = np.ascontiguousarray(a)
        arrays[f"in_{name}"] = a
        io[name] = nc.dram_tensor(f"in_{name}", a.shape, mybir.dt.from_np(a.dtype), kind="ExternalInput").ap()
    io["out"] = nc.dram_tensor("out_0", (NODES, FEAT), F32, kind="ExternalOutput").ap()
    build(nc, io)
    r = run_bass_kernel_spmd(nc, [arrays], core_ids=[0])
    return r.results[0]["out_0"]
```

```python
from contextlib import ExitStack

import numpy as np

import concourse.bass as bass
from concourse import mybir

F32 = mybir.dt.float32
I32 = mybir.dt.int32
ALU = mybir.AluOpType
ACT = mybir.ActivationFunctionType
AXX = mybir.AxisListType.X

P = 128
NODES = 6250
EDGES = 100000
FEAT = 256
NODE_TILES = -(-NODES // P)
NODES_PAD = NODE_TILES * P
FULL_TILES = NODES // P
TAIL_ROWS = NODES - FULL_TILES * P
CHUNKS = -(-EDGES // P)
EDGES_PAD = CHUNKS * P
STEPS = CHUNKS + NODE_TILES - 1
GROUP = 16
GROUPS = -(-STEPS // GROUP)
LOT = 7
LOTS = NODE_TILES // LOT
STEPS_PAD = GROUPS * GROUP
STEP_BLOCKS = -(-STEPS_PAD // P)
HEADS0 = 8
HEAD0_DIM = FEAT // HEADS0
HEADS3 = 4
OUT3 = 64
HIDDEN = 512
ROW3 = 2 * OUT3 + 2 * HEADS3
ROW0 = FEAT + HEADS0
ACC_W = FEAT + 2 * HEADS0
LOW = -1.0e38
LN_EPS = 1e-5
JUNK_NODE = NODES_PAD - 1


class Engine:

    def __init__(self, sem):
        self.sem, self.count, self.queue, self.seen = sem, 0, [], {}

    def wait(self, *tokens):
        for sem, value in tokens:
            if self.seen.get(id(sem), 0) < value:
                self.seen[id(sem)] = value
                self.queue.append(lambda e, s=sem, v=value: e.wait_ge(s, v))

    def do(self, make, after=()):
        self.wait(*after)
        self.count += 1
        self.queue.append(lambda e: make(e).then_inc(self.sem, 1))
        return (self.sem, self.count)

    def dma(self, make, done, after=()):
        self.wait(*after)
        done[1] += 16
        self.queue.append(lambda e: make(e).then_inc(done[0], 16))
        return (done[0], done[1])

    def plain(self, make):
        self.queue.append(make)

    def last(self):
        return (self.sem, self.count)

    def replay(self, e):
        for step in self.queue:
            step(e)


def pipeline(n, stages):
    for i in range(n + len(stages) - 1):
        for k in range(len(stages) - 1, -1, -1):
            if 0 <= i - k < n:
                for part in stages[k]:
                    part(i - k)


def build(nc, io):
    ctx = ExitStack()
    with ctx:
        def sb(name, width, dt=F32, rows=P):
            return ctx.enter_context(nc.sbuf_tensor(name, [rows, width], dt))

        def sem(name):
            return ctx.enter_context(nc.semaphore(name))

        def dram(name, shape, dt=F32):
            return nc.dram_tensor(name, shape, dt, kind="Internal").ap()

        reg_x = sb("reg_x", max(NODE_TILES * FEAT, 3 * GROUP * (ROW0 + 1)))
        reg_acc = sb("reg_acc", NODE_TILES * ACC_W)
        reg_a = sb("reg_a", 3 * GROUP * ROW3)
        reg_b = sb("reg_b", 7488)
        reg_w = sb("reg_w", 7 * HIDDEN)
        src_idx = sb("src_idx", STEPS_PAD, I32)
        dst_loc = sb("dst_loc", STEPS_PAD)
        edge_w = sb("edge_w", STEPS_PAD)
        attr0 = sb("attr0", STEPS_PAD)
        attr1 = sb("attr1", STEPS_PAD)
        cap = sb("cap", STEPS_PAD)[:, :]
        tile_row = sb("tile_row", STEPS_PAD, I32, rows=1)
        group_row = sb("group_row", NODE_TILES, I32, rows=1)
        ident = sb("ident", P)
        iota_row = sb("iota_row", P)
        adst = sb("adst", NODE_TILES * HEADS0)
        dinv = sb("dinv", NODE_TILES)
        small = sb("small", 512)
        psum = [ctx.enter_context(nc.psum_tensor(f"bank{k}", [P, 512], F32)) for k in range(8)]

        tab_h0 = dram("tab_h0", [NODES_PAD, ROW0])
        tab_x1 = dram("tab_x1", [NODES_PAD, FEAT])
        tab_h2 = dram("tab_h2", [NODES_PAD, FEAT])
        tab_x2 = dram("tab_x2", [NODES_PAD, FEAT])
        tab_h3 = dram("tab_h3", [NODES_PAD, ROW3])
        tile_dram = dram("tile_dram", [STEP_BLOCKS * P, 1], I32)
        group_dram = dram("group_dram", [NODE_TILES, 1], I32)

        pe, dve, act, pool, sp = (Engine(sem(f"s_{n}")) for n in ("pe", "dve", "act", "pool", "sp"))
        engines = (pe, dve, act, pool, sp)
        load_done = [sem("s_load"), 0]
        load2_done = [sem("s_load2"), 0]
        store_done = [sem("s_store"), 0]
        table_done = [sem("s_table"), 0]
        n_gather = 12
        gather_done = [[sem(f"s_gather{k}"), 0] for k in range(n_gather)]
        group_done = [[sem(f"s_group{k}"), 0] for k in range(3)]
        lot_done = [[sem(f"s_lot{k}"), 0] for k in range(LOTS)]
        stage_done = [[sem(f"s_stage{k}"), 0] for k in range(2)]
        counters = [load_done, load2_done, store_done, table_done] + stage_done + gather_done + group_done + lot_done

        def phase_end():
            tokens = [e.last() for e in engines] + [tuple(c) for c in counters]
            for e in engines:
                e.wait(*tokens)

        def tt(out, a, b, op, after=(), eng=None):
            return (eng or dve).do(lambda e: e.tensor_tensor(out, a, b, op), after)

        def ts(out, a, s1, s2, op0, op1=None, after=()):
            if op1 is None:
                return dve.do(lambda e: e.tensor_scalar(out, a, s1, None, op0), after)
            return dve.do(lambda e: e.tensor_scalar(out, a, s1, s2, op0, op1), after)

        def stt(out, a, s, b, op0, op1, after=()):
            return dve.do(lambda e: e.scalar_tensor_tensor(out=out, in0=a, scalar=s, in1=b, op0=op0, op1=op1), after)

        def copy(eng, out, a, after=()):
            if eng is act:
                return act.do(lambda e: e.copy(out, a), after)
            return eng.do(lambda e: e.tensor_copy(out, a), after)

        def activate(out, a, fn, after=(), **kw):
            return act.do(lambda e: e.activation(out, a, fn, **kw), after)

        def mm(out, lhs_t, rhs, start=True, stop=True, after=()):
            return pe.do(lambda e: e.matmul(out, lhs_t, rhs, start=start, stop=stop), after)

        def transpose(out, a, after=()):
            n = a.shape[0]
            return pe.do(lambda e: e.transpose(out, a, ident[0:n, 0:n]), after)

        def load(out, a, after=()):
            return sp.dma(lambda e: e.dma_start(out, a), load_done, after)

        def gather(out, table, t, done, after=()):
            return pool.dma(lambda e: e.indirect_dma_start(
                out, None, table, bass.IndirectOffsetOnAxis(ap=src_idx[:, t:t + 1], axis=0)), done, after)

        def node_rows(table, a, b):
            return table.rearrange("(t p) f -> p t f", p=P)[:, a:b, :]

        def bcast(ap, axis, shape):
            return ap.unsqueeze(axis).to_broadcast(shape)

        x_sb = reg_x[:, 0:NODE_TILES * FEAT].rearrange("p (t f) -> p t f", f=FEAT)
        acc = reg_acc[:, :].rearrange("p (t f) -> p t f", f=ACC_W)

        x_rows = io["x"][0:FULL_TILES * P, :].rearrange("(t p) f -> p t f", p=P)

        def load_x():
            t = dve.do(lambda e: e.memset(x_sb[:, FULL_TILES, :], 0.0))
            for a in range(LOTS):
                full = slice(a * LOT, min((a + 1) * LOT, FULL_TILES))
                sp.dma(lambda e, full=full: e.dma_start(x_sb[:, full, :], x_rows[:, full, :]), lot_done[a])
            sp.dma(lambda e: e.dma_start(x_sb[0:TAIL_ROWS, FULL_TILES, :], io["x"][FULL_TILES * P:NODES, :]),
                   lot_done[LOTS - 1], [t])
            return [tuple(c) for c in lot_done]

        small_i = small[:, 0:P].bitcast(I32)
        t_iota = pool.do(lambda e: e.iota(small_i, pattern=[[1, P]], base=0, channel_multiplier=0))
        t_part = pool.do(lambda e: e.iota(small[:, P:P + 1].bitcast(I32), pattern=[[0, 1]], base=0,
                                          channel_multiplier=1))
        step_i = small[:, 144:144 + STEP_BLOCKS].bitcast(I32)
        t_step = pool.do(lambda e: e.iota(step_i, pattern=[[P, STEP_BLOCKS]], base=0, channel_multiplier=1))
        chunk_i = reg_a[0:1, 0:CHUNKS].bitcast(I32)
        t_chunk = pool.do(lambda e: e.iota(chunk_i, pattern=[[1, CHUNKS]], base=1, channel_multiplier=0))
        copy(dve, iota_row[:, :], small_i, [t_iota])
        part = small[:, 130:131]
        t = copy(dve, part, small[:, P:P + 1].bitcast(I32), [t_part])
        ts(ident[:, :], iota_row[:, :], part, None, ALU.is_equal, after=[t])
        step_no = small[:, 160:160 + STEP_BLOCKS]
        copy(dve, step_no, step_i, [t_step])
        ones_row = small[0:1, 200:200 + P]
        dve.do(lambda e: e.memset(ones_row, 1.0))

        last_dst = reg_a[0:1, 800:800 + CHUNKS].bitcast(I32)
        ends = io["edge_ints"][:, 2 * P - 1:2 * P].rearrange("c k -> k c")
        t_ends = sp.dma(lambda e: e.dma_start(last_dst, ends, allow_slow_non_contiguous=True), load2_done)
        w0 = reg_w[:, 0:2 * ACC_W].rearrange("p (k f) -> p k f", k=2)
        att = reg_w[:, 2 * ACC_W:2 * ACC_W + 2 * FEAT]
        load(w0[:, :, 0:FEAT], io["w0"].rearrange("(k p) f -> p k f", p=P))
        for n, name in enumerate(("att_src", "att_dst")):
            load(att[:, n * FEAT:(n + 1) * FEAT], io[name].partition_broadcast(P))
        t_x = load_x()
        last_tile = reg_a[0:1, 1600:1600 + CHUNKS].bitcast(I32)
        t = dve.do(lambda e: e.tensor_scalar(last_tile, last_dst, 7, None, ALU.arith_shift_right), [t_ends])
        bound = reg_a[0:1, 2400:2400 + CHUNKS]
        t = tt(bound, last_tile, chunk_i, ALU.add, [t, t_chunk])
        half = CHUNKS // 2
        mm(psum[0][:, 0:half], ones_row, bound[:, 0:half], after=[t])
        t = mm(psum[1][:, 0:CHUNKS - half], ones_row, bound[:, half:CHUNKS])
        bounds = reg_a[:, 3200:3200 + CHUNKS]
        copy(dve, bounds[:, 0:half], psum[0][:, 0:half], [t])
        t = copy(dve, bounds[:, half:CHUNKS], psum[1][:, 0:CHUNKS - half])
        chunk_of = small[:, 170:170 + STEP_BLOCKS]
        hits = reg_a[:, 4000:4000 + CHUNKS]
        for b in range(STEP_BLOCKS):
            t = dve.do(lambda e, b=b: e.tensor_scalar(hits, bounds, step_no[:, b:b + 1], 0.0, ALU.is_le, ALU.add,
                                                      accum_out=chunk_of[:, b:b + 1]), [t])
        t = ts(chunk_of, chunk_of, float(CHUNKS - 1), None, ALU.min, after=[t])
        tile_of = small[:, 180:180 + STEP_BLOCKS]
        chunk_idx = small[:, 190:190 + STEP_BLOCKS].bitcast(I32)
        t_idx = copy(dve, chunk_idx, chunk_of, [t])
        t = tt(tile_of, step_no, chunk_of, ALU.subtract, [t])
        first_node = small[:, 330:330 + STEP_BLOCKS]
        t_first = ts(first_node, tile_of, float(P), None, ALU.mult, after=[t])
        tile_i = small[:, 340:340 + STEP_BLOCKS].bitcast(I32)
        t = ts(tile_i, tile_of, float(NODE_TILES - 1), None, ALU.min, after=[t])
        t = sp.dma(lambda e: e.dma_start(tile_dram.rearrange("(b p) k -> p (b k)", p=P), tile_i,
                                              allow_slow_non_contiguous=True), store_done, [t])
        t_tile_row = sp.dma(lambda e: e.dma_start(tile_row[:, :], tile_dram[0:STEPS_PAD, :].rearrange("s k -> k s")),
                   load2_done, [t])

        NI, NF = 4, 3
        at_flts, at_conv, at_flags = STEP_BLOCKS * NI * P, STEP_BLOCKS * (NI + NF) * P, STEP_BLOCKS * (2 * NI + NF) * P
        ints = reg_acc[:, 0:at_flts].bitcast(I32).rearrange("p (b f) -> p b f", b=STEP_BLOCKS)
        flts = reg_acc[:, at_flts:at_conv].rearrange("p (b f) -> p b f", b=STEP_BLOCKS)
        conv = reg_acc[:, at_conv:at_flags].rearrange("p (b f) -> p b f", b=STEP_BLOCKS)
        for b in range(STEP_BLOCKS):
            for out, table in ((ints[:, b, :], io["edge_ints"]), (flts[:, b, :], io["edge_floats"])):
                t_rows = pool.dma(lambda e, out=out, table=table, b=b: e.indirect_dma_start(
                    out, None, table, bass.IndirectOffsetOnAxis(ap=chunk_idx[:, b:b + 1], axis=0)),
                    table_done, [t_idx])

        def score_weights(att_row, where, after):
            prod = reg_w[:, 1568:1568 + 2 * FEAT].rearrange("p (k f) -> p k f", k=2)
            t = tt(prod, w0[:, :, 0:FEAT], bcast(att_row, 1, [P, 2, FEAT]), ALU.mult, after)
            return dve.do(lambda e: e.tensor_reduce(
                w0[:, :, where:where + HEADS0], prod.rearrange("p k (h d) -> p k h d", h=HEADS0), AXX, ALU.add), [t])

        t = score_weights(att[:, 0:FEAT], FEAT, [tuple(load_done)])
        t_w0 = score_weights(att[:, FEAT:2 * FEAT], FEAT + HEADS0, [t])

        def matmul_stages(source, k_chunks, weights, width, turned, ready, banks=(0, 1, 2, 3)):
            t_turn, t_copy, t_mm, used = {}, {}, {}, {}
            two = turned.rearrange("p (s f) -> p s f", s=2)

            def turn(j):
                for k in range(k_chunks):
                    t_turn[j] = transpose(psum[banks[j % 2]][:, k * P:(k + 1) * P], source(j)[:, k * P:(k + 1) * P],
                                          ready(j) + ([t_copy[j - 2]] if j >= 2 else []))

            def keep(j):
                t_copy[j] = copy(act, two[:, j % 2, :], psum[banks[j % 2]][:, 0:k_chunks * P],
                                 [t_turn[j]] + ([t_mm[j - 2]] if j >= 2 else []))

            def multiply(j):
                for k in range(k_chunks):
                    t_mm[j] = mm(psum[banks[2 + j % 2]][:, 0:width], two[:, j % 2, k * P:(k + 1) * P], weights[:, k, :],
                                 k == 0, k == k_chunks - 1,
                                 [t_copy[j]] + ([used[j - 2]] if j >= 2 else []))

            return turn, keep, multiply, t_mm, used, banks

        turn, keep, multiply, t_mm, used, banks = matmul_stages(
            lambda j: x_sb[:, j, :], 2, w0, ACC_W, reg_w[:, 1056:1056 + 4 * P], lambda j: [t_w0, t_x[j // LOT]])
        stage = reg_b[:, 3520:3520 + 2 * LOT * ROW0].rearrange("p (s t f) -> p s t f", s=2, f=ROW0)

        def keep_h(j):
            a, bank = j // LOT, psum[banks[2 + j % 2]]
            stored = [tuple(stage_done[a % 2])] if a >= 2 else []
            copy(dve, stage[:, a % 2, j % LOT, :], bank[:, 0:ROW0], [t_mm[j]] + stored)
            used[j] = copy(dve, adst[:, j * HEADS0:(j + 1) * HEADS0], bank[:, FEAT + HEADS0:ACC_W])
            if j % LOT == LOT - 1:
                sp.dma(lambda e: e.dma_start(node_rows(tab_h0, a * LOT, (a + 1) * LOT), stage[:, a % 2]),
                       stage_done[a % 2], [used[j]])

        def store_lot(table, view, a, after):
            return sp.dma(lambda e: e.dma_start(node_rows(table, a * LOT, (a + 1) * LOT),
                                                view[:, a * LOT:(a + 1) * LOT, :]), store_done, after)

        masks = reg_b[:, 0:2 * STEPS_PAD].rearrange("p (k t) -> p k t", k=2)
        start_mask, end_mask = masks[:, 0, :], masks[:, 1, :]
        dst_before, dst_behind, flag, is_valid = (
            reg_acc[:, at_flags + 128 + k * STEPS_PAD:at_flags + 128 + (k + 1) * STEPS_PAD] for k in range(4))
        run_masks = reg_b[0:1, 2 * STEPS_PAD:4 * STEPS_PAD].rearrange("p (k t) -> p k t", k=2)
        head_starts = reg_b[0:1, 4 * STEPS_PAD:4 * STEPS_PAD + GROUPS]
        carried = reg_b[:, 4 * STEPS_PAD + 64:4 * STEPS_PAD + 64 + GROUPS]
        tok, freed = {}, {}

        tile_f = reg_a[0:1, 800:800 + STEPS_PAD]
        tiles_all = reg_a[:, 1700:1700 + STEPS_PAD]
        step_half = STEPS_PAD // 2
        n_steps = small[:, 134:135]
        n_steps_i = small[:, 135:136].bitcast(I32)
        tile_hits = reg_a[:, 4000:4000 + STEPS_PAD]

        def tiles_to_all():
            t = copy(dve, tile_f, tile_row[:, :], [t_tile_row])
            for k in range(2):
                tok["b"] = mm(psum[4 + k][:, 0:step_half], ones_row, tile_f[:, k * step_half:(k + 1) * step_half],
                              after=[t])

        def last_groups():
            for k in range(2):
                freed[4 + k] = t = copy(dve, tiles_all[:, k * step_half:(k + 1) * step_half],
                                        psum[4 + k][:, 0:step_half], [tok["b"]])
            t = dve.do(lambda e: e.tensor_scalar(tile_hits, tiles_all, part, 0.0, ALU.is_le, ALU.add,
                                                 accum_out=n_steps), [t])
            t = ts(n_steps_i, n_steps, -1.0, None, ALU.add, after=[t])
            t = dve.do(lambda e: e.tensor_scalar(n_steps_i, n_steps_i, GROUP.bit_length() - 1, None,
                                                 ALU.arith_shift_right), [t])
            t = sp.dma(lambda e: e.dma_start(group_dram, n_steps_i[0:NODE_TILES, :]), store_done, [t])
            sp.dma(lambda e: e.dma_start(group_row[:, :], group_dram.rearrange("s k -> k s")), load2_done, [t])

        def as_floats(b):
            tok["src"] = copy(dve, conv[:, b, 0:P], ints[:, b, 0:P], [t_rows])
            tok["dst"] = ts(conv[:, b, P:4 * P], ints[:, b, P:4 * P], first_node[:, b:b + 1], None, ALU.subtract,
                            after=[t_first])

        def turn_rows(b, n):
            w = min(P, STEPS_PAD - b * P)
            attributes = flts[:, b, 0:2 * P].rearrange("p (j k) -> p k j", k=2)
            rows, out = ((conv[:, b, 0:P], src_idx), (conv[:, b, P:2 * P], dst_loc),
                         (conv[:, b, 2 * P:3 * P], dst_before), (conv[:, b, 3 * P:4 * P], dst_behind),
                         (attributes[:, 0, :], attr0), (attributes[:, 1, :], attr1),
                         (flts[:, b, 2 * P:3 * P], edge_w))[n]
            k = 4 + (b * 7 + n) % 4
            t = transpose(psum[k][:, 0:P], rows, [tok["dst"], t_rows] + ([freed[k]] if k in freed else []))
            freed[k] = tok["tab"] = copy(dve, out[:, b * P:b * P + w], psum[k][:, 0:w], [t])

        def clear_middle():
            pool.do(lambda e: e.memset(reg_acc[:, 2240:at_flags + 128], 0.0), [tok["tab"]])

        def valid():
            t = ts(flag, dst_loc[:, :], 0.0, None, ALU.is_ge, after=[tok["tab"]])
            tok["v"] = stt(is_valid, dst_loc[:, :], float(P), flag, ALU.is_lt, ALU.mult, [t])

        def caps():
            tok["v"] = ts(cap, is_valid, -2.0 * LOW, LOW, ALU.mult, ALU.add, after=[tok["v"]])

        def node_ends(other, mask):
            t = tt(flag, dst_loc[:, :], other, ALU.not_equal, [tok["v"]])
            tok["v"] = stt(mask, flag, LOW, is_valid, ALU.mult, ALU.mult, [t])

        counts = reg_acc[:, 0:2 * STEPS_PAD]
        ones_col = reg_acc[:, 2 * STEPS_PAD:2 * STEPS_PAD + 1]

        def count_ends():
            t = ts(counts, reg_b[:, 0:2 * STEPS_PAD], 0.0, None, ALU.is_lt, after=[tok["v"]])
            t = dve.do(lambda e: e.memset(ones_col, 1.0), [t])
            for k in range(4):
                tok["c"] = mm(psum[4 + k][0:1, 0:step_half], ones_col, counts[:, k * step_half:(k + 1) * step_half],
                              after=[t])

        def step_ends():
            for k in range(4):
                t = ts(reg_b[0:1, 2 * STEPS_PAD + k * step_half:2 * STEPS_PAD + (k + 1) * step_half],
                       psum[4 + k][0:1, 0:step_half], 1.0, LOW, ALU.min, ALU.mult, after=[tok["c"]])
            t = copy(dve, head_starts, run_masks[:, 0, ::GROUP], [t])
            dve.do(lambda e: e.memset(run_masks[:, 0, ::GROUP], LOW), [t])
            dve.do(lambda e: e.memset(run_masks[:, 1, GROUP - 1::GROUP], LOW))

        def carried_on():
            goes_on = reg_acc[0:1, 2000:2000 + GROUPS]
            going = reg_acc[0:1, 2100:2100 + GROUPS]
            t = ts(goes_on, start_mask[0:1, ::GROUP], 0.0, None, ALU.is_equal, after=[dve.last()])
            t = tt(goes_on, goes_on, is_valid[0:1, ::GROUP], ALU.mult, [t])
            t = stt(going, dst_loc[0:1, ::GROUP], 1.0, goes_on, ALU.add, ALU.mult, [t])
            t = ts(going, going, -1.0, None, ALU.add, after=[t])
            t = mm(psum[4][:, 0:GROUPS], ones_row, going, after=[t])
            t = ts(carried, psum[4][:, 0:GROUPS], part, None, ALU.is_equal, after=[t])
            pool.do(lambda e: e.memset(reg_acc[:, 0:2240], 0.0), [t])
            pool.do(lambda e: e.memset(reg_acc[:, at_flags + 128:], 0.0), [t])

        beside = {4: [tiles_to_all], 6: [last_groups]}
        pieces = []
        for b in range(STEP_BLOCKS):
            pieces.append([lambda b=b: as_floats(b), lambda b=b: turn_rows(b, 0)])
            pieces += [[lambda b=b, n=n: turn_rows(b, n), lambda b=b, n=n: turn_rows(b, n + 1)] for n in (1, 3, 5)]
        pieces += [[clear_middle, valid], [caps], [lambda: node_ends(dst_before, start_mask)],
                   [lambda: node_ends(dst_behind, end_mask)], [count_ends], [step_ends], [carried_on]]
        first_tile = 12
        for n, piece in enumerate(pieces):
            beside[first_tile + n] = piece

        def piece_beside(j):
            for part_of_it in beside.get(j, []):
                part_of_it()

        pipeline(NODE_TILES, [[piece_beside], [turn], [keep], [multiply], [keep_h]])
        assert max(beside) < NODE_TILES
        phase_end()

        regs = {}

        def load_tiles(eng, t0, n):
            def make(e):
                if eng not in regs:
                    regs[eng] = [e.alloc_register(f"tile{k}") for k in range(16)]
                e.load(regs[eng][0:n], tile_row[0:1, t0:t0 + n])
            eng.plain(make)

        def tile_value(eng, e, t):
            return e.snap(regs[eng][t % 16], min_val=0, max_val=NODE_TILES - 1)

        def distances(out, t, after):
            return activate(out, iota_row[:, :], ACT.Abs, after, scale=-1.0, bias=dst_loc[:, t:t + 1])

        def one_hots(out, after):
            return activate(out, out, ACT.Relu, after, scale=-1.0, bias=1.0)

        def scan(out, mask, data, initial, after=()):
            return dve.do(lambda e: e.tensor_tensor_scan(out, mask, data, initial, ALU.add, ALU.max), after)

        def leaky(v, after):
            return stt(v, v, 0.2, v, ALU.mult, ALU.max, after)

        n_hot, n_bank, lag = 4, 6, 2
        rows = reg_a[:, 0:n_gather * FEAT].rearrange("p (s f) -> p s f", f=FEAT)
        hots = reg_a[:, n_gather * FEAT:n_gather * FEAT + n_hot * P].rearrange("p (s f) -> p s f", f=P)
        def add_product(i, bank, width, after):
            if i % 16 == 0:
                load_tiles(dve, i, 16)

            def make(e):
                a = reg_acc[:, bass.DynSlice(tile_value(dve, e, i) * ACC_W, width)]
                return e.tensor_tensor(a, a, bank[:, 0:width], ALU.add)
            return dve.do(make, after)

        def edge_pass(table, kind):
            t_got, t_hot, t_mm, t_add = {}, {}, {}, {}

            def fetch(i):
                free = t_mm.get(i - n_gather)
                t_got[i] = gather(rows[:, i % n_gather, :], table, i, gather_done[i % n_gather],
                                  [free] if free else [])

            def prepare(i):
                hot, row = hots[:, i % n_hot, :], rows[:, i % n_gather, :]
                free = [t_mm[i - n_hot]] if i >= n_hot else []
                if kind == "weighted":
                    t_hot[i] = ts(hot, iota_row[:, :], dst_loc[:, i:i + 1], edge_w[:, i:i + 1], ALU.is_equal,
                                  ALU.mult, after=free)
                else:
                    t_hot[i] = ts(hot, iota_row[:, :], dst_loc[:, i:i + 1], None, ALU.is_equal, after=free)

            def product(i):
                bank = psum[i % n_bank]
                hot = hots[:, i % n_hot, :]
                rhs = rows[:, i % n_gather, :]
                after = [t_hot[i], t_got[i]] + ([t_add[i - n_bank]] if i >= n_bank else [])
                t_mm[i] = mm(bank[:, 0:FEAT], hot, rhs, after=after)

            def add(i):
                t_add[i] = add_product(i, psum[i % n_bank], FEAT, [t_mm[i]] + ([t_add[i - 1]] if i else []))

            for i in range(STEPS + lag):
                if i < STEPS:
                    fetch(i)
                    prepare(i)
                    product(i)
                if i >= lag:
                    add(i - lag)
            phase_end()

        sums = acc[:, :, 0:FEAT]
        n_stat = 2 * LOT

        def norm_rings(at):
            return (reg_b[:, at:at + n_stat * 6].rearrange("p (t k) -> p t k", k=6),
                    reg_b[:, at + n_stat * 6:at + n_stat * 8].rearrange("p (t k) -> p t k", k=2),
                    reg_b[:, at + n_stat * 8:at + n_stat * 9], reg_b[:, at + n_stat * 9:at + n_stat * 10])

        rings_a, rings_b = norm_rings(6700), norm_rings(6850)
        recip = reg_b[:, 7000:7000 + NODE_TILES * HEADS0].rearrange("p (t h) -> p t h", h=HEADS0)
        eps_col = small[:, 440:441]
        dve.do(lambda e: e.memset(eps_col, LN_EPS))

        def lot(view, a):
            return view[:, a * LOT:(a + 1) * LOT, :]

        def norm_stages(size, src, out, ready, rings=rings_a):
            stats, moments, rstd, shift = rings
            t_moment, t_root, t_inverse, t_norm = {}, {}, {}, {}

            def tiles(i):
                return range(i * size, (i + 1) * size)

            def ring(i):
                return slice(i * size % n_stat, i * size % n_stat + size)

            def moment(i):
                for j in tiles(i):
                    t = dve.do(lambda e, j=j: e.bn_stats(stats[:, j % n_stat, :], src(j)), ready(i))
                for j in tiles(i):
                    t_moment[i] = dve.do(lambda e, j=j: e.bn_aggr(moments[:, j % n_stat, :], stats[:, j % n_stat, :]),
                                         [t])

            def root(i):
                t_root[i] = activate(rstd[:, ring(i)], moments[:, ring(i), 1], ACT.Sqrt,
                                     [t_moment[i]] + [t_norm[k] for k in [i - n_stat // size] if k >= 0],
                                     bias=eps_col)

            def inverse(i):
                t = dve.do(lambda e: e.reciprocal(rstd[:, ring(i)], rstd[:, ring(i)]), [t_root[i]])
                t_inverse[i] = stt(shift[:, ring(i)], moments[:, ring(i), 0], -1.0, rstd[:, ring(i)], ALU.mult,
                                   ALU.mult, [t])

            def scale(i):
                for j in tiles(i):
                    k = j % n_stat
                    t_norm[i] = activate(out(j), src(j), ACT.Identity, [t_inverse[i]], scale=rstd[:, k:k + 1],
                                         bias=shift[:, k:k + 1])

            return [moment, root], [inverse, scale], t_norm

        def load_vectors(names, at):
            out = []
            for name in names:
                n = io[name].shape[-1]
                load(reg_w[:, at:at + n], io[name].partition_broadcast(P))
                out.append(reg_w[:, at:at + n])
                at += n
            return out

        def all_heads(a, factors, n_heads, after):
            v = lot(sums, a).rearrange("p t (h d) -> p t h d", h=n_heads)
            return tt(v, v, bcast(lot(factors, a), 3, [P, LOT, n_heads, FEAT // n_heads]), ALU.mult, after)

        def heads_pass():
            S, H, D = GROUP, HEADS0, HEAD0_DIM
            width = FEAT + H + 1
            rows0 = reg_x[:, 0:3 * S * width].rearrange("p (s f) -> p s f", f=width)
            hots = reg_a[:, 0:2 * S * P].rearrange("p (s f) -> p s f", f=P)
            hots_t = reg_a[:, 2 * S * P:2 * S * P + 1024].rearrange("p (s f) -> p s f", s=2)
            at_b = [4 * STEPS_PAD + 128]

            def take(width, rows=P):
                at_b[0] += width
                return reg_b[0:rows, at_b[0] - width:at_b[0]]

            upright = take(3 * P)
            turned3 = take(3 * P)
            first = take(2 * P)
            second = take(2 * P)
            dst_part = take(P)
            both = take(2 * P)
            begin_col = take(2)
            node_both = take(2 * H)
            shrink = take(H)
            step_masks, tails, states, begins = (take(2 * P, rows=1) for _ in range(4))
            assert at_b[0] <= 7488
            level = small[0:1, 400:400 + 4 * H].rearrange("p (k f) -> p k f", k=2)
            t_i0 = dve.do(lambda e: e.memset(level[:, 0, :], LOW))
            t_i1 = dve.do(lambda e: e.memset(begins, LOW))
            t_i2 = dve.do(lambda e: e.memset(rows0[:, :, ROW0:width], 1.0))
            n_bank, lag = 4, 3
            bank_t, bank_3, bank_d, bank_c = (psum[4], psum[5]), psum[6][:, 0:3 * P], psum[6][:, 3 * P:4 * P], psum[7]
            t_got, t_rhs, t_mm, t_add, t_weight, t_shrink, t_hot, t_scaled = {}, {}, {}, {}, {}, {}, {}, {}
            t_turned, t_kept, t_exp, t_level = {}, {}, {}, {}
            t_level[0] = t_i0

            def fetch(g):
                for t in range(g * S, (g + 1) * S):
                    free = [t_mm[t - 3 * S]] if g >= 3 else []
                    t_got[g] = gather(rows0[:, t % (3 * S), 0:ROW0], tab_h0, t, group_done[g % 3], free)

            def chain(g):
                block = rows0[:, g % 3 * S:(g % 3 + 1) * S, :]
                cols = slice(g * S, (g + 1) * S)
                tok = {}
                sh = "p (s h) -> p s h"

                def distance(k):
                    for t in (g * S + k, g * S + k + 1):
                        tok["a"] = distances(hots[:, t % (2 * S), :], t, [t_mm[t - 2 * S]] if g >= 2 else [])

                def hot(c):
                    a = (g * S + 4 * c) % (2 * S)
                    t_hot[g, c] = one_hots(hots[:, a:a + 4, :], [tok["a"]])

                def hot_turn(c):
                    for k in range(4):
                        t_turned[c] = transpose(bank_t[c % 2][:, k * P:(k + 1) * P],
                                                hots[:, (g * S + 4 * c + k) % (2 * S), :],
                                                [t_hot[g, c]] + ([t_kept[c % 2]] if c % 2 in t_kept else []))

                def hot_keep(c):
                    t_kept[c % 2] = copy(act, hots_t[:, c % 2, :], bank_t[c % 2][:, :],
                                         [t_turned[c]] + ([t_exp[c % 2]] if c % 2 in t_exp else []))

                def dst_mm(c):
                    if c == 0:
                        load_tiles(pe, g * S, S)
                    for k in range(4):
                        t = g * S + 4 * c + k
                        t_exp[c % 2] = pe.do(lambda e, t=t, c=c, k=k: e.matmul(
                            bank_d[:, t % S * H:(t % S + 1) * H], hots_t[:, c % 2, k * P:(k + 1) * P],
                            adst[:, bass.DynSlice(tile_value(pe, e, t) * H, H)], start=True, stop=True),
                            [t_kept[c % 2]] + ([t_part[0]] if t_part else []))

                def upright_masks():
                    tok["k"] = copy(act, step_masks.rearrange("p (k h s) -> p k h s", k=2, h=H),
                                    bcast(run_masks[:, :, cols], 2, [1, 2, H, S]), [t_level[g]])
                    tok["m"] = copy(act, upright[:, 0:2 * P].rearrange("p (k s h) -> p k s h", k=2, h=H),
                                    bcast(masks[:, :, cols], 3, [P, 2, S, H]), [t_u[0]] if t_u else [])
                    tok["s"] = tt(upright[:, 2 * P:3 * P].rearrange(sh, h=H), block[:, :, FEAT:ROW0],
                                  bcast(cap[:, cols], 2, [P, S, H]), ALU.min, [t_got[g]])

                def turn3():
                    for k in range(3):
                        tok["3"] = transpose(bank_3[:, k * P:(k + 1) * P], upright[:, k * P:(k + 1) * P],
                                             [tok["m"], tok["s"]])

                def keep3():
                    tok["3"] = copy(act, turned3, bank_3[:, 0:3 * P], [tok["3"]] + t_second)

                def first_round():
                    scan(first[:, 0:P], turned3[:, 0:P], turned3[:, 2 * P:3 * P], LOW, [tok["3"]])
                    tok["f"] = scan(first[:, P:2 * P][:, ::-1], turned3[:, P:2 * P][:, ::-1],
                                    turned3[:, 2 * P:3 * P][:, ::-1], LOW)

                def turn_tails():
                    for k in range(2):
                        tok["r"] = transpose(bank_c[0:1, k * P:(k + 1) * P], first[:, P - 1 + k:P + k], [tok["f"]])

                def keep_tails():
                    tok["r"] = copy(act, tails.rearrange("p (k h s) -> p k h s", k=2, h=H),
                                    bank_c[0:1, 0:2 * P].rearrange("p (k s h) -> p k h s", k=2, h=H), [tok["r"]])

                def over_steps():
                    ft = tails[:, 0:P].rearrange("p (h s) -> p h s", h=H)[:, :, 0]
                    t = stt(ft, level[:, g % 2, 0:H], head_starts[:, g:g + 1], ft, ALU.add, ALU.max,
                            [tok["r"], t_level[g]])
                    scan(states[:, P:2 * P][:, ::-1], step_masks[:, P:2 * P][:, ::-1], tails[:, P:2 * P][:, ::-1], LOW,
                         [tok["k"]])
                    tok["o"] = scan(states[:, 0:P], step_masks[:, 0:P], tails[:, 0:P], LOW, [t])

                def hand_on():
                    st = states.rearrange("p (k h s) -> p k s h", k=2, h=H)
                    be = begins.rearrange("p (k s h) -> p k s h", k=2, h=H)
                    copy(act, be[:, 0, 1:S, :], st[:, 0, 0:S - 1, :], [tok["o"]])
                    copy(act, be[:, 1, 0:S - 1, :], st[:, 1, 1:S, :])
                    tok["b"] = copy(act, be[:, 0, 0, :], level[:, g % 2, 0:H])
                    tok["l"] = tt(level[:, g % 2, H:2 * H], level[:, g % 2, 0:H], st[:, 1, 0, :], ALU.max, [tok["o"]])
                    t_level[g + 1] = copy(dve, level[:, (g + 1) % 2, 0:H], st[:, 0, S - 1, :])

                def turn_begins():
                    for k in range(2):
                        transpose(bank_c[:, 256 + k:257 + k], begins[:, k * P:(k + 1) * P], [tok["b"], t_i1])
                    tok["c"] = mm(bank_c[:, 264:264 + 2 * H], ones_row, level[:, g % 2, :], after=[tok["l"]])

                def keep_begins():
                    tok["c"] = copy(act, begin_col, bank_c[:, 256:258], [tok["c"]])

                def keep_part():
                    tok["d"] = t_part_new = copy(act, dst_part, bank_d[:, 0:S * H], [t_exp[1]])
                    t_part[:] = [t_part_new]

                def node_levels():
                    def make(e):
                        if "head" not in regs:
                            regs["head"] = e.alloc_register("head_tile")
                        e.load(regs["head"], tile_row[0:1, g * S:g * S + 1])
                        v = e.snap(regs["head"], min_val=0, max_val=NODE_TILES - 1)
                        return e.tensor_tensor(node_both.rearrange("p (k h) -> p k h", k=2),
                                               bank_c[:, 264:264 + 2 * H].rearrange("p (k h) -> p k h", k=2),
                                               bcast(adst[:, bass.DynSlice(v * H, H)], 1, [P, 2, H]), ALU.add)
                    tok["n"] = dve.do(make, [tok["c"]])

                def second_round():
                    scan(second[:, 0:P], turned3[:, 0:P], turned3[:, 2 * P:3 * P], begin_col[:, 0:1], [tok["c"]])
                    tok["x"] = scan(second[:, P:2 * P][:, ::-1], turned3[:, P:2 * P][:, ::-1],
                                    turned3[:, 2 * P:3 * P][:, ::-1], begin_col[:, 1:2])
                    t_second[:] = [tok["x"]]

                def larger():
                    tok["n"] = leaky(node_both, [tok["n"]])
                    tok["x"] = tt(second[:, 0:P], second[:, 0:P], second[:, P:2 * P], ALU.max, [tok["x"]])
                    tok["n"] = tt(shrink, node_both[:, 0:H], node_both[:, H:2 * H], ALU.subtract, [tok["n"]])
                    tok["e"] = activate(shrink, shrink, ACT.Exp, [tok["n"]])

                def turn_larger():
                    tok["x"] = transpose(bank_c[:, 3 * P:4 * P], second[:, 0:P], [tok["x"]])
                    tok["u"] = tt(both[:, 0:P], upright[:, 2 * P:3 * P], dst_part, ALU.add, [tok["d"]])
                    t_u[:] = [tok["u"]]

                def add_dst():
                    tok["u"] = tt(both[:, P:2 * P], bank_c[:, 3 * P:4 * P], dst_part, ALU.add, [tok["x"]])
                    tok["n"] = ts(shrink, shrink, -1.0, carried[:, g:g + 1], ALU.add, ALU.mult, after=[tok["e"]])

                def bend():
                    tok["u"] = leaky(both, [tok["u"]])
                    t_shrink[g] = ts(shrink, shrink, 1.0, None, ALU.add, after=[tok["n"]])

                def below():
                    tok["u"] = tt(both[:, 0:P], both[:, 0:P], both[:, P:2 * P], ALU.subtract, [tok["u"]])

                def exps():
                    t_weight[g] = activate(block[:, :, FEAT:ROW0], both[:, 0:P].rearrange(sh, h=H), ACT.Exp,
                                           [tok["u"], t_i2])

                def c(make, *args):
                    return lambda: make(*args)

                return [
                    ([upright_masks, c(distance, 0)], []),
                    ([turn3, c(distance, 2), c(hot, 0)], [keep3]),
                    ([c(distance, 4)], [c(hot_turn, 0), c(hot_keep, 0)]),
                    ([first_round, c(distance, 6), c(hot, 1)], []),
                    ([turn_tails, c(distance, 8)], [c(hot_turn, 1), keep_tails, c(hot_keep, 1), c(dst_mm, 0)]),
                    ([c(distance, 10), c(hot, 2)], []),
                    ([over_steps, c(distance, 12)], [hand_on, c(hot_turn, 2), c(hot_keep, 2), c(dst_mm, 1)]),
                    ([c(distance, 14), c(hot, 3)], [turn_begins]),
                    ([keep_begins], [c(hot_turn, 3), c(hot_keep, 3), c(dst_mm, 2)]),
                    ([], []),
                    ([], [c(dst_mm, 3)]),
                    ([node_levels, second_round, larger, keep_part], []),
                    ([turn_larger], []),
                    ([add_dst, bend], []),
                    ([below, exps], []),
                ]

            t_part, t_u, t_second = [], [], []

            def rescale(g):
                i = g * S
                load_tiles(dve, i, 16)

                def at(e, a, b):
                    return reg_acc[:, bass.DynSlice(tile_value(dve, e, i) * ACC_W + a, b - a)]

                def sums(e):
                    v = at(e, 0, FEAT).rearrange("p (h d) -> p h d", h=H)
                    return e.tensor_tensor(v, v, bcast(shrink, 2, [P, H, D]), ALU.mult)

                def denominators(e):
                    v = at(e, FEAT, FEAT + H)
                    return e.tensor_tensor(v, v, shrink, ALU.mult)
                dve.do(sums, [t_shrink[g], t_add[i - 1]])
                t_scaled[g] = dve.do(denominators)

            def prepare(i):
                g = i // S
                v = rows0[:, i % (3 * S), 0:FEAT].rearrange("p (h d) -> p h d", h=H)
                t_rhs[i] = tt(v, v, bcast(rows0[:, i % (3 * S), FEAT:ROW0], 2, [P, H, D]), ALU.mult, [t_weight[g]])

            def product(i):
                bank, hot = psum[i % n_bank], hots[:, i % (2 * S), :]
                t_mm[i] = mm(bank[:, 0:width], hot, rows0[:, i % (3 * S), :],
                             after=[t_rhs[i]] + ([t_add[i - n_bank]] if i >= n_bank else []))

            def add(i):
                g = i // S
                fresh = g and i % S == 0
                if fresh:
                    rescale(g)
                before = [t_scaled[g]] if fresh else [t_add[i - 1]] if i else []
                t_add[i] = add_product(i, psum[i % n_bank], width, [t_mm[i]] + before)

            fetch(0)
            fetch(1)
            for ahead, behind in chain(0):
                for link in ahead + behind:
                    link()
            for g in range(GROUPS):
                if g + 2 < GROUPS:
                    fetch(g + 2)
                steps = chain(g + 1) if g + 1 < GROUPS else []
                for k in range(S):
                    i = g * S + k
                    ahead, behind = steps[k] if k < len(steps) else ([], [])
                    prepare(i)
                    for link in ahead:
                        link()
                    product(i)
                    for link in behind:
                        link()
                    if i >= lag:
                        add(i - lag)
            for i in range(STEPS_PAD - lag, STEPS_PAD):
                add(i)
            phase_end()

        (bias0,) = load_vectors(["bias0"], 0)
        heads_pass()
        t_x = load_x()
        t = ts(dinv[:, :], acc[:, :, FEAT + HEADS0], 1.0, None, ALU.add)
        t_d = activate(dinv[:, :], dinv[:, :], ACT.Sqrt, [t])
        t = ts(recip, acc[:, :, FEAT:FEAT + HEADS0], 1e-16, None, ALU.add)
        t_recip = dve.do(lambda e: e.reciprocal(recip, recip), [t])
        t_dinv = dve.do(lambda e: e.reciprocal(dinv[:, :], dinv[:, :]), [t_d])
        t_mean, t_biased, t_x1 = {}, {}, {}

        def mean0(a):
            t_mean[a] = all_heads(a, recip, HEADS0, [t_recip])

        def bias_0(a):
            t_biased[a] = tt(lot(sums, a), lot(sums, a), bcast(bias0, 1, [P, LOT, FEAT]), ALU.add, [t_mean[a]], pool)

        def residual0(a):
            t_x1[a] = stt(lot(x_sb, a), lot(sums, a), 0.0, lot(x_sb, a), ALU.max, ALU.add, [t_biased[a], t_x[a]])

        norm0, scale0, t_norm0 = norm_stages(LOT, lambda j: x_sb[:, j, :], lambda j: x_sb[:, j, :], lambda a: [t_x1[a]])

        def degree0(a):
            for j in range(a * LOT, (a + 1) * LOT):
                t = act.do(lambda e, j=j: e.mul(sums[:, j, :], x_sb[:, j, :], dinv[:, j:j + 1]),
                           [t_norm0[a], t_dinv])
            store_lot(tab_x1, sums, a, [t])

        pipeline(LOTS, [[mean0, bias_0], [residual0], norm0, scale0 + [degree0]])
        phase_end()

        w1 = reg_w[:, 0:2 * HIDDEN].rearrange("p (k f) -> p k f", k=2)
        w2 = reg_w[:, 2 * HIDDEN:4 * HIDDEN].rearrange("p (k f) -> p k f", k=4)
        load(w1, io["w1"].rearrange("(k p) f -> p k f", p=P))
        load(w2, io["w2"].rearrange("(k p) f -> p k f", p=P))
        bias1, gamma1, beta1 = load_vectors(["b1", "gamma1", "beta1"], 4 * HIDDEN)
        edge_pass(tab_x1, "plain")
        turned = reg_a[:, 0:4 * P]
        turn_1, keep_1, multiply_1, t_mm_1, used_1, banks_1 = matmul_stages(
            lambda j: sums[:, j, :], 2, w1, HIDDEN, turned, lambda j: [])
        hid = reg_a[:, 1024:1024 + 4 * HIDDEN].rearrange("p (s f) -> p s f", s=4)
        t_stat, t_hid, t_turn2 = {}, {}, {}

        stats, moments, rstd, _ = rings_a

        def hidden_in(j):
            h, k = hid[:, j % 4, :], j % n_stat
            used_1[j] = t = stt(h, psum[banks_1[2 + j % 2]][:, :], dinv[:, j:j + 1], bias1, ALU.mult, ALU.add,
                                [t_mm_1[j]] + ([t_turn2[j - 4]] if j >= 4 else []))
            t = dve.do(lambda e: e.bn_stats(stats[:, k, :], h), [t])
            t = dve.do(lambda e: e.bn_aggr(moments[:, k, :], stats[:, k, :]), [t])
            t_stat[j] = activate(rstd[:, k:k + 1], moments[:, k, 1:2], ACT.Sqrt, [t], bias=eps_col)

        def hidden_norm(j):
            h, k = hid[:, j % 4, :], j % n_stat
            t = dve.do(lambda e: e.reciprocal(rstd[:, k:k + 1], rstd[:, k:k + 1]), [t_stat[j]])
            t = ts(h, h, moments[:, k, 0:1], rstd[:, k:k + 1], ALU.subtract, ALU.mult, after=[t])
            t = tt(h, h, gamma1, ALU.mult, [t])
            t = tt(h, h, beta1, ALU.add, [t])
            t_hid[j] = activate(h, h, ACT.Relu, [t])

        turned2 = reg_a[:, 3072:3072 + 8 * P]
        turn2, keep2, multiply2, t_mm2, used2, banks2 = matmul_stages(
            lambda j: hid[:, j % 4, :], 4, w2, FEAT, turned2, lambda j: [t_hid[j]], banks=(4, 5, 6, 7))

        def turn2_noted(j):
            turn2(j)
            t_turn2[j] = pe.last()

        def hidden_out(j):
            used2[j] = act.do(lambda e: e.mul(sums[:, j, :], psum[banks2[2 + j % 2]][:, 0:FEAT], dinv[:, j:j + 1]),
                              [t_mm2[j]])
            if j % LOT == LOT - 1:
                store_lot(tab_h2, sums, j // LOT, [used2[j]])

        pipeline(NODE_TILES, [[turn_1], [keep_1], [multiply_1], [hidden_in], [hidden_norm], [turn2_noted], [keep2],
                              [multiply2], [hidden_out]])
        phase_end()

        bias2, gamma2, beta2 = load_vectors(["b2", "gamma2", "beta2"], 0)
        wl2 = reg_w[:, 3 * FEAT:5 * FEAT].rearrange("p (k f) -> p k f", k=2)
        load(wl2, io["w_l2"].rearrange("(k p) f -> p k f", p=P))
        (bias_l2,) = load_vectors(["b_l2"], 5 * FEAT)
        raw = reg_w[0:OUT3, 6 * FEAT:8 * FEAT].rearrange("p (d f) -> p d f", d=2)
        load(raw[:, 0, :], io["w_fwd"])
        load(raw[:, 1, :], io["w_rev"])
        attn_row = reg_w[0:HEADS3, 8 * FEAT:8 * FEAT + OUT3]
        load(attn_row, io["attn"])
        edge_pass(tab_h2, "plain")

        turner = reg_w[0:OUT3, 2112:2112 + OUT3 + HEADS3]
        w3 = reg_w[:, 2200:2200 + 2 * ROW3].rearrange("p (k f) -> p k f", k=2)
        t = transpose(psum[0][0:OUT3, 0:HEADS3], attn_row)
        copy(dve, turner[:, OUT3:OUT3 + HEADS3], psum[0][0:OUT3, 0:HEADS3], [t])
        t = copy(dve, turner[:, 0:OUT3], ident[0:OUT3, 0:OUT3])
        for d in range(2):
            for k in range(2):
                bank = psum[1 + 2 * d + k]
                t_w = mm(bank[:, 0:OUT3 + HEADS3], raw[:, d, k * P:(k + 1) * P], turner, after=[t])
                copy(dve, w3[:, k, d * OUT3:(d + 1) * OUT3], bank[:, 0:OUT3], [t_w])
                copy(dve, w3[:, k, 2 * OUT3 + d * HEADS3:2 * OUT3 + (d + 1) * HEADS3], bank[:, OUT3:OUT3 + HEADS3])

        t_deg2, t_bias2, t_gamma2, t_beta2, t_res2 = {}, {}, {}, {}, {}

        def degree2(a):
            for j in range(a * LOT, (a + 1) * LOT):
                t_deg2[a] = act.do(lambda e, j=j: e.mul(sums[:, j, :], sums[:, j, :], dinv[:, j:j + 1]))

        def bias_2(a):
            t_bias2[a] = tt(lot(sums, a), lot(sums, a), bcast(bias2, 1, [P, LOT, FEAT]), ALU.add, [t_deg2[a]], pool)

        norm_g, scale_g, t_norm_g = norm_stages(LOT, lambda j: sums[:, j, :], lambda j: sums[:, j, :], lambda a: [t_bias2[a]])

        def gamma_2(a):
            t_gamma2[a] = tt(lot(sums, a), lot(sums, a), bcast(gamma2, 1, [P, LOT, FEAT]), ALU.mult, [t_norm_g[a]])

        def beta_2(a):
            t_beta2[a] = tt(lot(sums, a), lot(sums, a), bcast(beta2, 1, [P, LOT, FEAT]), ALU.add, [t_gamma2[a]], pool)

        def residual2(a):
            t_res2[a] = stt(lot(x_sb, a), lot(sums, a), 0.0, lot(x_sb, a), ALU.max, ALU.add, [t_beta2[a]])
            pool.do(lambda e: e.memset(lot(sums, a), 0.0), [t_res2[a]])

        norm_x, scale_x, t_norm_x = norm_stages(LOT, lambda j: x_sb[:, j, :], lambda j: x_sb[:, j, :], lambda a: [t_res2[a]],
                                                  rings_b)

        def finish2(a):
            store_lot(tab_x2, x_sb, a, [t_norm_x[a]])

        pipeline(LOTS, [[part] for part in [degree2, bias_2] + norm_g + scale_g + [gamma_2, beta_2, residual2] +
                        norm_x + scale_x + [finish2]])
        phase_end()

        edge_pass(tab_x2, "weighted")
        turn_2, keep_2, multiply_2, t_mm_2, used_2, banks_2 = matmul_stages(
            lambda j: sums[:, j, :], 2, wl2, FEAT, turned, lambda j: [])
        biased = reg_a[:, 1024:1024 + 2 * FEAT].rearrange("p (s f) -> p s f", s=2)
        t_res_l2 = {}

        def l2_out(j):
            v = biased[:, j % 2, :]
            used_2[j] = t = tt(v, psum[banks_2[2 + j % 2]][:, 0:FEAT], bias_l2, ALU.add, [t_mm_2[j]])
            t_res_l2[j] = stt(x_sb[:, j, :], v, 0.0, x_sb[:, j, :], ALU.max, ALU.add, [t])
            pool.do(lambda e: e.memset(acc[:, j, 0:FEAT + HEADS3], 0.0), [t_mm_2[j]])

        norm_l2, scale_l2, t_norm_l2 = norm_stages(1, lambda j: x_sb[:, j, :], lambda j: x_sb[:, j, :],
                                                   lambda j: [t_res_l2[j]])
        turn_3, keep_3, multiply_3, t_mm_3, used_3, banks_3 = matmul_stages(
            lambda j: x_sb[:, j, :], 2, w3, ROW3, reg_a[:, 2048:2048 + 4 * P], lambda j: [t_norm_l2[j]],
            banks=(4, 5, 6, 7))
        table3 = reg_b[:, 0:NODE_TILES * ROW3].rearrange("p (t f) -> p t f", f=ROW3)

        def l3_keep(j):
            used_3[j] = copy(dve, table3[:, j, :], psum[banks_3[2 + j % 2]][:, 0:ROW3], [t_mm_3[j]])
            if j % LOT == LOT - 1:
                store_lot(tab_h3, table3, j // LOT, [used_3[j]])

        pipeline(NODE_TILES, [[turn_2], [keep_2], [multiply_2], [l2_out], norm_l2, scale_l2, [turn_3], [keep_3],
                              [multiply_3], [l3_keep]])
        phase_end()

        def mix_pass():
            rows3 = reg_a[:, 0:3 * GROUP * ROW3].rearrange("p (s f) -> p s f", f=ROW3)
            rings = reg_b[:, :]
            hots = rings[:, 3100:3100 + 12 * P].rearrange("p (s f) -> p s f", s=12)
            reverse = rings[:, 512:512 + 4 * OUT3].rearrange("p (s f) -> p s f", s=4)
            message = rings[:, 768:768 + 4 * OUT3].rearrange("p (s f) -> p s f", s=4)
            scaled = rings[:, 4700:4700 + 4 * (FEAT + HEADS3)].rearrange("p (s f) -> p s f", s=4)
            ghw = [P, GROUP, HEADS3]
            weight = rings[:, 2048:2048 + 3 * GROUP * HEADS3].rearrange("p (g t h) -> p g t h", g=3, h=HEADS3)
            part_score = rings[:, 2304:2304 + 2 * GROUP * HEADS3].rearrange("p (k t h) -> p k t h", k=2, h=HEADS3)
            top = rings[:, 2500:2500 + HEADS3]
            shrink = rings[:, 2510:2510 + HEADS3]
            run_top = rings[0:HEADS3, 2520:2520 + GROUPS + 1]
            diag = rings[0:HEADS3, 2580:2580 + HEADS3]
            ones4 = rings[0:HEADS3, 2600:2600 + P]
            tops = rings[:, 2800:2800 + GROUPS * HEADS3].rearrange("p (g h) -> p g h", h=HEADS3)
            bank_c = psum[7]
            dve.do(lambda e: e.memset(ones4, 1.0))
            t_init = dve.do(lambda e: e.memset(run_top[:, 0:1], LOW))
            width = FEAT + HEADS3
            t_got, t_rhs, t_mm, t_add, t_weight, t_shrink, t_hot = {}, {}, {}, {}, {}, {}, {}
            t_scaled, t_wcopy, t_msg = {}, {}, {}

            def fetch(g):
                for t in range(g * GROUP, (g + 1) * GROUP):
                    free = [t_msg[t - 3 * GROUP]] if g >= 3 else []
                    t_got[g] = gather(rows3[:, t % (3 * GROUP), :], tab_h3, t, group_done[g % 3], free)

            def chain(g):
                block = rows3[:, g % 3 * GROUP:(g % 3 + 1) * GROUP, 2 * OUT3:]
                cols = slice(g * GROUP, (g + 1) * GROUP)
                w = weight[:, g % 3]
                tok = {}

                def scores():
                    tt(part_score[:, 0], block[:, :, 0:HEADS3], bcast(attr0[:, cols], 2, ghw), ALU.mult, [t_got[g]])
                    tok["s"] = tt(part_score[:, 1], block[:, :, HEADS3:], bcast(attr1[:, cols], 2, ghw), ALU.mult)

                def total():
                    tok["s"] = tt(w, part_score[:, 0], part_score[:, 1], ALU.add, [tok["s"]])

                def bend():
                    tok["s"] = leaky(w.rearrange("p t h -> p (t h)"), [tok["s"]])

                def slot_top():
                    tok["t"] = dve.do(lambda e: e.tensor_reduce(top, w.rearrange("p t h -> p h t"), AXX, ALU.max),
                                      [tok["s"]])

                def turn_top():
                    tok["t"] = transpose(bank_c[0:HEADS3, 0:P], top, [tok["t"]])

                def all_top():
                    tok["t"] = dve.do(lambda e: e.tensor_reduce(run_top[:, g + 1:g + 2], bank_c[0:HEADS3, 0:P], AXX,
                                                                ALU.max), [tok["t"], t_init])

                def so_far():
                    tok["t"] = tt(run_top[:, g + 1:g + 2], run_top[:, g:g + 1], run_top[:, g + 1:g + 2], ALU.max,
                                  [tok["t"]])

                def on_diagonal():
                    tok["t"] = ts(diag, ident[0:HEADS3, 0:HEADS3], run_top[:, g + 1:g + 2], None, ALU.mult,
                                  after=[tok["t"]])

                def to_all():
                    tok["t"] = mm(bank_c[:, 256:256 + HEADS3], ones4, diag, after=[tok["t"]])

                def keep_top():
                    tok["t"] = copy(dve, tops[:, g, :], bank_c[:, 256:256 + HEADS3], [tok["t"]])

                def below():
                    t = tt(w, w, bcast(tops[:, g, :], 1, ghw), ALU.subtract, [tok["t"]])
                    if g:
                        t = tt(shrink, tops[:, g - 1, :], tops[:, g, :], ALU.subtract)
                    tok["t"] = t

                def exps():
                    wf = w.rearrange("p t h -> p (t h)")
                    t_weight[g] = activate(wf, wf, ACT.Exp, [tok["t"]])
                    if g:
                        t_shrink[g] = activate(shrink, shrink, ACT.Exp, [tok["t"]])

                return [[scores], [total], [bend], [slot_top], [turn_top], [], [all_top], [so_far], [on_diagonal],
                        [to_all], [], [keep_top], [below], [exps]]

            def rescale(g):
                i = g * GROUP
                load_tiles(dve, i, 16)

                def at(e, a, b):
                    return reg_acc[:, bass.DynSlice(tile_value(dve, e, i) * ACC_W + a, b - a)]

                def sums(e):
                    v = at(e, 0, FEAT).rearrange("p (h d) -> p h d", h=HEADS3)
                    return e.tensor_tensor(v, v, bcast(shrink, 2, [P, HEADS3, OUT3]), ALU.mult)

                def denominators(e):
                    v = at(e, FEAT, width)
                    return e.tensor_tensor(v, v, shrink, ALU.mult)
                dve.do(sums, [t_shrink[g], t_add[i - 1]])
                t_scaled[g] = dve.do(denominators)

            def hot(i):
                t = distances(hots[:, i % 12, :], i, [t_mm[i - 12]] if i >= 12 else [])
                if i % 4 == 3:
                    t_hot[i // 4] = one_hots(hots[:, (i - 3) % 12:(i - 3) % 12 + 4, :], [t])

            def mix(i):
                s, row = i % 4, rows3[:, i % (3 * GROUP), :]
                t = act.do(lambda e: e.mul(reverse[:, s, :], row[:, OUT3:2 * OUT3], attr1[:, i:i + 1]),
                           [t_got[i // GROUP]] + ([t_msg[i - 4]] if i >= 4 else []))
                t_msg[i] = stt(message[:, s, :], row[:, 0:OUT3], attr0[:, i:i + 1], reverse[:, s, :], ALU.mult,
                               ALU.add, [t])

            def prepare(i):
                s, g = i % 4, i // GROUP
                free = [t_mm[i - 4]] if i >= 4 else []
                t_wcopy[i] = copy(act, scaled[:, s, FEAT:width], weight[:, g % 3, i % GROUP, :],
                                  [t_weight[g]] + free)
                t_rhs[i] = tt(scaled[:, s, 0:FEAT].rearrange("p (h d) -> p h d", h=HEADS3),
                              bcast(message[:, s, :], 1, [P, HEADS3, OUT3]),
                              bcast(weight[:, g % 3, i % GROUP, :], 2, [P, HEADS3, OUT3]), ALU.mult,
                              [t_msg[i], t_weight[g]] + free)
                if i + 1 < STEPS_PAD:
                    mix(i + 1)

            def product(i):
                t_mm[i] = mm(psum[i % n_bank][:, 0:width], hots[:, i % 12, :], scaled[:, i % 4, :],
                             after=[t_hot[i // 4], t_rhs[i], t_wcopy[i]] +
                             ([t_add[i - n_bank]] if i >= n_bank else []))

            def add(i):
                g = i // GROUP
                if g and i % GROUP == 0:
                    rescale(g)
                t_add[i] = add_product(i, psum[i % n_bank], width,
                                       [t_mm[i], t_scaled[g] if i % GROUP == 0 and g else dve.last()]
                                       if i % GROUP == 0 else [t_mm[i], t_add[i - 1]])

            fetch(0)
            fetch(1)
            for links in chain(0):
                for link in links:
                    link()
            for i in range(8):
                hot(i)
            mix(0)
            for g in range(GROUPS):
                if g + 2 < GROUPS:
                    fetch(g + 2)
                steps = chain(g + 1) if g + 1 < GROUPS else []
                for k in range(GROUP):
                    i = g * GROUP + k
                    prepare(i)
                    if k < len(steps):
                        for link in steps[k]:
                            link()
                    if i + 8 < STEPS_PAD:
                        hot(i + 8)
                    product(i)
                    if i >= lag:
                        add(i - lag)
            for i in range(STEPS_PAD - lag, STEPS_PAD):
                add(i)
            phase_end()
            return tops

        tops = mix_pass()
        factor = reg_a[:, 0:NODE_TILES * HEADS3].rearrange("p (t h) -> p t h", h=HEADS3)
        factor_r = reg_a[:, 256:256 + NODE_TILES * HEADS3].rearrange("p (t h) -> p t h", h=HEADS3)
        tops_flat = tops.rearrange("p g h -> p (g h)")
        group_regs = []

        def pick(d):
            def make(e):
                if not group_regs:
                    group_regs.extend(e.alloc_register(f"group{k}") for k in range(8))
                if d % 8 == 0:
                    n = min(8, NODE_TILES - d)
                    e.load(group_regs[0:n], group_row[0:1, d:d + n])
                v = e.snap(group_regs[d % 8], min_val=0, max_val=GROUPS - 1)
                return e.tensor_copy(factor[:, d, :], tops_flat[:, bass.DynSlice(v * HEADS3, HEADS3)])
            return dve.do(make)

        for d in range(NODE_TILES):
            t = pick(d)
        t = tt(factor, factor, bcast(tops[:, GROUPS - 1, :], 1, [P, NODE_TILES, HEADS3]), ALU.subtract, [t])
        t = activate(factor, factor, ACT.Exp, [t])
        den = acc[:, :, FEAT:FEAT + HEADS3]
        t = tt(den, den, factor, ALU.mult, [t])
        t = ts(den, den, 1e-10, None, ALU.add, after=[t])
        t = dve.do(lambda e: e.reciprocal(factor_r, den), [t])
        t = tt(factor, factor, factor_r, ALU.mult, [t])
        t_factor = t
        out_rows = io["out"][0:FULL_TILES * P, :].rearrange("(t p) f -> p t f", p=P)
        t_mean3, t_res3 = {}, {}

        def mean3(a):
            t_mean3[a] = all_heads(a, factor, HEADS3, [t_factor])

        def residual3(a):
            t_res3[a] = tt(lot(x_sb, a), lot(sums, a), lot(x_sb, a), ALU.add, [t_mean3[a]], (pool, dve)[a % 2])

        norm3, scale3, t_norm3 = norm_stages(LOT, lambda j: x_sb[:, j, :], lambda j: x_sb[:, j, :], lambda a: [t_res3[a]])

        def finish3(a):
            full = slice(a * LOT, min((a + 1) * LOT, FULL_TILES))
            sp.dma(lambda e: e.dma_start(out_rows[:, full, :], x_sb[:, full, :]), store_done, [t_norm3[a]])
            if a == LOTS - 1:
                sp.dma(lambda e: e.dma_start(io["out"][FULL_TILES * P:NODES, :], x_sb[0:TAIL_ROWS, FULL_TILES, :]),
                       store_done)

        pipeline(LOTS, [[mean3], [residual3], norm3, scale3 + [finish3]])
        sp.wait(tuple(store_done))

        block = ctx.enter_context(nc.Block())

        @block.tensor
        def _(e):
            pe.replay(e)

        @block.vector
        def _(e):
            dve.replay(e)

        @block.scalar
        def _(e):
            act.replay(e)

        @block.gpsimd
        def _(e):
            pool.replay(e)

        @block.sync
        def _(e):
            sp.replay(e)


def kernel(x, src, dst, edge_attr_2, edge_weight, L0_gnn_W, L0_gnn_att_src, L0_gnn_att_dst, L0_gnn_bias, L1_gnn_W1,
           L1_gnn_b1, L1_gnn_gamma1, L1_gnn_beta1, L1_gnn_W2, L1_gnn_b2, L1_gnn_gamma2, L1_gnn_beta2, L2_gnn_W,
           L2_gnn_b, L3_gnn_W_forward, L3_gnn_W_reverse, L3_gnn_attn_forward):
    import concourse.bacc as bacc
    from concourse.bass_utils import run_bass_kernel_spmd

    fill = EDGES_PAD - EDGES
    src, dst = np.asarray(src), np.asarray(dst)
    attr, weight = np.asarray(edge_attr_2), np.asarray(edge_weight)
    none = np.full(1, -1, dst.dtype)
    dst_pad = np.concatenate([dst, np.full(fill, JUNK_NODE, dst.dtype)])
    edge_ints = np.concatenate([v.reshape(CHUNKS, P) for v in (
        np.concatenate([src, src[-fill:]]), dst_pad, np.concatenate([none, dst_pad[:-1]]),
        np.concatenate([dst_pad[1:], none]))], axis=1)
    edge_floats = np.concatenate([np.concatenate([attr, attr[-fill:]]).reshape(CHUNKS, 2 * P),
                                  np.concatenate([weight, weight[-fill:]]).reshape(CHUNKS, P)], axis=1)
    ins = {
        "x": x, "edge_ints": edge_ints, "edge_floats": edge_floats,
        "w0": np.asarray(L0_gnn_W).reshape(FEAT, FEAT), "att_src": np.asarray(L0_gnn_att_src).reshape(FEAT),
        "att_dst": np.asarray(L0_gnn_att_dst).reshape(FEAT), "bias0": L0_gnn_bias,
        "w1": L1_gnn_W1, "b1": L1_gnn_b1, "gamma1": L1_gnn_gamma1, "beta1": L1_gnn_beta1,
        "w2": L1_gnn_W2, "b2": L1_gnn_b2, "gamma2": L1_gnn_gamma2, "beta2": L1_gnn_beta2,
        "w_l2": L2_gnn_W, "b_l2": L2_gnn_b, "w_fwd": L3_gnn_W_forward, "w_rev": L3_gnn_W_reverse,
        "attn": np.asarray(L3_gnn_attn_forward).reshape(HEADS3, OUT3),
    }
    nc = bacc.Bacc("TRN2", target_bir_lowering=False, num_devices=1)
    arrays, io = {}, {}
    for name, a in ins.items():
        a = np.ascontiguousarray(a)
        arrays[f"in_{name}"] = a
        io[name] = nc.dram_tensor(f"in_{name}", a.shape, mybir.dt.from_np(a.dtype), kind="ExternalInput").ap()
    io["out"] = nc.dram_tensor("out_0", (NODES, FEAT), F32, kind="ExternalOutput").ap()
    build(nc, io)
    r = run_bass_kernel_spmd(nc, [arrays], core_ids=[0])
    return r.results[0]["out_0"]
```
